# Optimizing a Trainium2 kernel written in Bass

```python
import numpy as np
import jax
import jax.numpy as jnp

def _softmax(x, axis=-1):
    return jax.nn.softmax(x, axis=axis)

def _gelu(x):
    return jax.nn.gelu(x, approximate=True)

def _silu(x):
    return jax.nn.silu(x)

def _sigmoid(x):
    return jax.nn.sigmoid(x)

def _layernorm(x, axis=-1, eps=1e-05):
    m = jnp.mean(x, axis=axis, keepdims=True)
    v = jnp.var(x, axis=axis, keepdims=True)
    return (x - m) / jnp.sqrt(v + eps)

def _scatter_add(tgt, idx, src, axis=0):
    return tgt.at[idx].add(src)

def _segment_sum(src, seg, n):
    return jax.ops.segment_sum(src, seg, n)
kernel_name = 'mk_adj_preln_d2_adj_r2_e678ea'

def setup_inputs(seed: int=0):
    np.random.seed(seed)
    _w = jnp.asarray

    def _rec_inputs():
        import jax
        import jax.numpy as jnp
        _gk = jax.random.key(seed)
        x = -0.0002928 + 1 * jax.random.normal(jax.random.fold_in(_gk, 1), (8192, 128), jnp.float32)
        _a = jax.random.bernoulli(jax.random.fold_in(_gk, 2), 0.00195312, (8192, 8192))
        _a = jnp.logical_or(_a, jnp.swapaxes(_a, -1, -2))
        _a = jnp.logical_or(_a, jnp.eye(8192, dtype=bool))
        _af = _a.astype(jnp.float32)
        _af = _af * jax.random.uniform(jax.random.fold_in(_gk, 3), (8192, 8192), jnp.float32, 0.05, 1)
        adj = _af
        return (x, adj)
    x, adj = _rec_inputs()

    def _L0_gnn_setup():
        import jax, jax.numpy as jnp
        import numpy as np
        EPS = 1e-05
        SLOPE = 0.01

        def _bn(x, gamma, beta):
            mu = jnp.mean(x, axis=0, keepdims=True)
            var = jnp.mean((x - mu) ** 2, axis=0, keepdims=True)
            return (x - mu) * jax.lax.rsqrt(var + EPS) * gamma + beta

        def _leaky(x):
            return jnp.where(x >= 0, x, SLOPE * x)
        key = jax.random.key(seed)
        ks = jax.random.split(key, 16)
        n_m, n_n, d, mf = (8192, 8192, 128, 2)
        h = 2 * d * mf

        def lin(k, fan_in, shape):
            b = 1.0 / np.sqrt(fan_in)
            return jax.random.uniform(k, shape, jnp.float32, -b, b)
        return {'M': jax.random.normal(ks[0], (n_m, d), jnp.float32), 'N': jax.random.normal(ks[1], (n_n, d), jnp.float32), 'adj_m2n': jax.random.uniform(ks[2], (n_n, n_m), jnp.float32), 'W_in': lin(ks[3], d, (d, d)), 'b_in': lin(ks[4], d, (d,)), 'g1': jnp.ones((2 * d,), jnp.float32), 'be1': jnp.zeros((2 * d,), jnp.float32), 'W1': lin(ks[5], 2 * d, (h, 2 * d)), 'b1': lin(ks[6], 2 * d, (h,)), 'g2': jnp.ones((h,), jnp.float32), 'be2': jnp.zeros((h,), jnp.float32), 'W2': lin(ks[7], h, (d, h)), 'b2': lin(ks[8], h, (d,))}
    _L0_gnn_all = _L0_gnn_setup()
    _L0_gnn_in = {k: v for k, v in _L0_gnn_all.items() if k in ('N', 'W_in', 'b_in', 'g1', 'be1', 'W1', 'b1', 'g2', 'be2', 'W2', 'b2')}
    del _L0_gnn_all

    def _L1_gnn_setup():
        import jax, jax.numpy as jnp
        import numpy as np
        N, IN_C, OUT_C = (4096, 128, 128)
        key = jax.random.key(seed)
        k1, k2, k3 = jax.random.split(key, 3)
        x = jax.random.normal(k1, (N, IN_C), dtype=jnp.float32)
        adj = jax.random.uniform(k2, (N, N), dtype=jnp.float32)
        limit = float(np.sqrt(6.0 / (IN_C + OUT_C)))
        weight = jax.random.uniform(k3, (IN_C, OUT_C), dtype=jnp.float32, minval=-limit, maxval=limit)
        bias = jnp.zeros((OUT_C,), dtype=jnp.float32)
        return {'x': x, 'adj': adj, 'weight': weight, 'bias': bias}
    _L1_gnn_all = _L1_gnn_setup()
    _L1_gnn_in = {k: v for k, v in _L1_gnn_all.items() if k in ('weight', 'bias')}
    del _L1_gnn_all
    return {'x': x, 'adj': adj, 'L0_gnn_N': _L0_gnn_in['N'], 'L0_gnn_W_in': _L0_gnn_in['W_in'], 'L0_gnn_b_in': _L0_gnn_in['b_in'], 'L0_gnn_g1': _L0_gnn_in['g1'], 'L0_gnn_be1': _L0_gnn_in['be1'], 'L0_gnn_W1': _L0_gnn_in['W1'], 'L0_gnn_b1': _L0_gnn_in['b1'], 'L0_gnn_g2': _L0_gnn_in['g2'], 'L0_gnn_be2': _L0_gnn_in['be2'], 'L0_gnn_W2': _L0_gnn_in['W2'], 'L0_gnn_b2': _L0_gnn_in['b2'], 'L1_gnn_weight': _L1_gnn_in['weight'], 'L1_gnn_bias': _L1_gnn_in['bias']}

def reference(x, adj, L0_gnn_N, L0_gnn_W_in, L0_gnn_b_in, L0_gnn_g1, L0_gnn_be1, L0_gnn_W1, L0_gnn_b1, L0_gnn_g2, L0_gnn_be2, L0_gnn_W2, L0_gnn_b2, L1_gnn_weight, L1_gnn_bias):
    import jax
    import jax.numpy as jnp

    def _L0_gnn_ref(M, N, adj_m2n, W_in, b_in, g1, be1, W1, b1, g2, be2, W2, b2):
        import jax, jax.numpy as jnp
        import numpy as np
        EPS = 1e-05
        SLOPE = 0.01

        def _bn(x, gamma, beta):
            mu = jnp.mean(x, axis=0, keepdims=True)
            var = jnp.mean((x - mu) ** 2, axis=0, keepdims=True)
            return (x - mu) * jax.lax.rsqrt(var + EPS) * gamma + beta

        def _leaky(x):
            return jnp.where(x >= 0, x, SLOPE * x)
        Mh = M @ W_in.T + b_in
        M2N = adj_m2n @ Mh
        x = jnp.concatenate([N, M2N], axis=1)
        x = _bn(x, g1, be1)
        x = _leaky(x @ W1.T + b1)
        x = _bn(x, g2, be2)
        x = _leaky(x @ W2.T + b2)
        return N + x

    def _L1_gnn_ref(x, adj, weight, bias):
        import jax, jax.numpy as jnp
        import numpy as np
        N, IN_C, OUT_C = (4096, 128, 128)
        deg = jnp.sum(adj, axis=1)
        d = deg ** (-0.5)
        d = jnp.where(jnp.isinf(d), 0.0, d)
        adj_norm = d[:, None] * adj * d[None, :]
        support = x @ weight
        out = adj_norm @ support + bias
        return out
    h = jnp.maximum(_layernorm(x, axis=-1), 0.0)
    x = x + _L0_gnn_ref(h, L0_gnn_N, adj, L0_gnn_W_in, L0_gnn_b_in, L0_gnn_g1, L0_gnn_be1, L0_gnn_W1, L0_gnn_b1, L0_gnn_g2, L0_gnn_be2, L0_gnn_W2, L0_gnn_b2)
    h = jnp.maximum(_layernorm(x, axis=-1), 0.0)
    x = x + _L1_gnn_ref(h, adj, L1_gnn_weight, L1_gnn_bias)
    return x

_drawn_inputs = setup_inputs


def setup_inputs(seed=0):
    import zlib

    import numpy as np

    out = dict(_drawn_inputs(seed))
    spreads = {'L0_gnn_g1': (1.0, 0.2),
     'L0_gnn_be1': (0.0, 0.743),
     'L0_gnn_g2': (1.0, 0.2),
     'L0_gnn_be2': (0.0, 0.377),
     'L1_gnn_bias': (0.0, 0.1)}
    factors = {'L0_gnn_b_in': 3.009, 'L0_gnn_b1': 7.853, 'L0_gnn_b2': 6.185}
    for name, (base, spread) in spreads.items():
        noise = np.random.default_rng([zlib.crc32(name.encode()), seed]).standard_normal(out[name].shape)
        drawn = base * np.exp(spread * noise) if base else spread * noise
        out[name] = jnp.asarray(drawn.astype(out[name].dtype))
    for name, factor in factors.items():
        out[name] = (out[name] * factor).astype(out[name].dtype)
    return out
```

```python
from contextlib import ExitStack

import concourse.bass as bass
from concourse import mybir

F32 = mybir.dt.float32
F32R = mybir.dt.float32r
ALU = mybir.AluOpType
ACT = mybir.ActivationFunctionType

P = 128
D = 128
NODES = 8192
H = 512
EPS = 1e-5
SLOPE = 0.01

BANK = 512
GROUP = 2048
GROUPS = NODES // GROUP
BANKS = GROUP // BANK
TILES = NODES // P
CHUNK = BANK // P
CHUNKS = NODES // BANK
RING = 4
TURNS = TILES // RING
KT = 2 * D // P
QT = H // P
PAIRS = 4

SCRATCH = 1024


def gnn_kernel(nc, adjT, x_rows, n_rows, nT, w_inT, b_in, g1, be1, w1T, b1, g2, be2, w2T, b2,
               weight, bias, out_rows, xn_dram):
    with ExitStack() as ctx:
        top = [-(-nc.sbuf_base // 64) * 64]

        def at(name, shape, dt=F32, offset=None):
            size = 4
            for n in shape[1:]:
                size *= n
            if offset is None:
                offset = top[0]
                top[0] += -(-size // 32) * 32
            return nc.alloc_sbuf_tensor_at(name, shape, dt, offset=offset)

        ring = at("ring", [P, RING, GROUP])
        m2nT = at("m2nT", [P, NODES])
        m2n_base = top[0] - 4 * NODES
        x1 = at("x1", [P, CHUNKS, CHUNK, D], offset=m2n_base)
        space = top[0]
        hid = at("hid", [P, CHUNKS, QT, BANK])
        mh = hid[:, :, 0, :]
        xr = hid[:, :, 1, :]
        nr = hid[:, :, 2, :]
        nTs = hid[:, :, 3, :]
        degacc = hid[:, 0:4, 2, :]
        parts = at("parts", [P, CHUNKS, QT, BANK], F32R, offset=space)
        v2hi, v2lo = parts[:, :, 0, :], parts[:, :, 1, :]
        half = 2 * BANK
        flat = parts[:, :, :, :].rearrange("p c q j -> p c (q j)")
        ahi = [flat[:, 4 * b:4 * b + 2, half:2 * half] for b in range(PAIRS)]
        alo = [flat[:, 4 * b + 2:4 * b + 4, half:2 * half] for b in range(PAIRS)]

        work = top[0]
        stage = at("stage", [P, RING, D])
        hn = at("hn", [P, CHUNK, D])
        hT = at("hT", [P, BANK])
        yT = at("yT", [P, BANK])
        spare = at("spare", [P, 2, BANK])
        stage_hi = at("stage_hi", [P, RING, D], F32R, offset=work)
        stage_lo = at("stage_lo", [P, RING, D], F32R, offset=work + 4 * BANK)
        sumT = at("sumT", [P, BANKS, BANK], offset=work + 8 * BANK)

        w_in_s = at("w_in_s", [P, D])
        w1_s = at("w1_s", [P, KT, H])
        w2_s = at("w2_s", [P, QT, D])
        w_s = at("w_s", [P, D])
        ident = at("ident", [P, P])
        b_in_s = at("b_in_s", [P, D])
        bias_s = at("bias_s", [P, D])
        g1_s = at("g1_s", [P, KT])
        be1_s = at("be1_s", [P, KT])
        b1_s = at("b1_s", [P, QT])
        g2_s = at("g2_s", [P, QT])
        be2_s = at("be2_s", [P, QT])
        b2_s = at("b2_s", [P, 1])
        ones = at("ones", [P, 1])
        mhalf = at("mhalf", [P, CHUNK])
        ln_bn = at("ln_bn", [P, CHUNK, 6])
        ln_mv = at("ln_mv", [P, CHUNK, 2])
        ln_neg = at("ln_neg", [P, TILES])
        ln_ve = at("ln_ve", [P, TILES])
        ln_rs = at("ln_rs", [P, TILES])
        ln_sh = at("ln_sh", [P, TILES])
        bn1_st = at("bn1_st", [P, KT, CHUNKS, 6])
        bn2_st = at("bn2_st", [P, QT, CHUNKS, 6])
        bn_mv = at("bn_mv", [P, QT, 2])
        bn_ve = at("bn_ve", [P, QT])
        bn_rs = at("bn_rs", [P, QT])
        bn_s = at("bn_s", [P, QT])
        bn_ms = at("bn_ms", [P, QT])
        bn_t = at("bn_t", [P, QT])
        c1 = at("c1", [P, QT])
        c2 = at("c2", [P, 1])
        tick = at("tick", [P, 1])
        deg = at("deg", [P, TILES])
        dzero = at("dzero", [P, TILES])
        dinv = at("dinv", [P, TILES])
        dbad = at("dbad", [P, TILES])
        dsc = at("dsc", [P, TILES])
        assert top[0] <= nc.sbuf_top, top[0]

        acc = ctx.enter_context(nc.psum_tensor("acc", [P, BANKS, BANK], F32))
        ps = [ctx.enter_context(nc.psum_tensor(f"ps{i}", [P, BANK], F32)) for i in range(4)]

        def sem(name):
            return ctx.enter_context(nc.semaphore(name))

        x_in, n_in, nT_in, w_in_l, xn_out, xn_in, stored = (
            sem(n) for n in ("x_in", "n_in", "nT_in", "w_in_l", "xn_out", "xn_in", "stored"))
        adj_in = [sem(f"adj_in{s}") for s in range(RING)]
        const_ok, ident_ok = sem("const_ok"), sem("ident_ok")
        ln_part, ln_var, ln_rstd, ln_shift = sem("ln_part"), sem("ln_var"), sem("ln_rstd"), sem("ln_shift")
        rows_norm, rows_turned, turned_kept, mh_made, mh_kept = (
            sem(n) for n in ("rows_norm", "rows_turned", "turned_kept", "mh_made", "mh_kept"))
        staged, tile_summed, deg_added = sem("staged"), sem("tile_summed"), sem("deg_added")
        m2n_kept, deg_clear, deg_made, deg_kept, bn1_seen = (
            sem(n) for n in ("m2n_kept", "deg_clear", "deg_made", "deg_kept", "bn1_seen"))
        xn_made = sem("xn_made")
        dve_step, pool_step = sem("dve_step"), sem("pool_step")
        bn_var, bn_rstd, shift_ok, cvec_made, scaled_ok = (
            sem(n) for n in ("bn_var", "bn_rstd", "shift_ok", "cvec_made", "scaled_ok"))
        z_made, z_biased, h_kept, h_seen = sem("z_made"), sem("z_biased"), sem("h_kept"), sem("h_seen")
        y_made, y_biased, y_kept, y_turned, x1_made = sem("y_made"), sem("y_biased"), sem("y_kept"), sem("y_turned"), sem("x1_made")
        deg_final, d_ok = sem("deg_final"), sem("d_ok")
        ln2_var, ln2_rstd, ln2_shift = sem("ln2_var"), sem("ln2_rstd"), sem("ln2_shift")
        rows2_norm, rows2_turned, turned2_kept, sup_made, hi_kept, lo_kept = (
            sem(n) for n in ("rows2_norm", "rows2_turned", "turned2_kept", "sup_made", "hi_kept", "lo_kept"))
        bias_added = sem("bias_added")
        staged2, split_hi, split_lo, tile_summed2 = (
            sem(n) for n in ("staged2", "split_hi", "split_lo", "tile_summed2"))
        sum_kept, sum_turned, out_made = sem("sum_kept"), sem("sum_turned"), sem("out_made")

        PASS = GROUPS * TILES

        def cols(t, n=1):
            return bass.ds(t, n)

        block = ctx.enter_context(nc.Block())

        @block.sync
        def _(sp):
            xr_d = x_rows.rearrange("p (c j) -> p c j", j=BANK)
            sp.dma_start(xr[:, 0:4, :], xr_d[:, 0:4, :]).then_inc(x_in, 16)
            sp.dma_start(w_in_s[:, :], w_inT).then_inc(w_in_l, 16)
            sp.dma_start(b_in_s[:, :], b_in.partition_broadcast(P)).then_inc(w_in_l, 16)

            def load_tile(tile, s):
                sp.dma_start(ring[:, s, :], adjT[tile]).then_inc(adj_in[s], 16)

            for s in range(RING):
                load_tile(s, s)
                if s == 0:
                    sp.wait_ge(x_in, 16)
                    sp.dma_start(xr[:, 4:CHUNKS, :], xr_d[:, 4:CHUNKS, :]).then_inc(x_in, 16)
            sp.dma_start(w1_s[:, :, :], w1T.rearrange("(k p) h -> p k h", p=P)).then_inc(w_in_l, 16)
            sp.dma_start(w2_s[:, :, :], w2T.rearrange("(k p) h -> p k h", p=P)).then_inc(w_in_l, 16)
            sp.dma_start(w_s[:, :], weight).then_inc(w_in_l, 16)
            sp.dma_start(bias_s[:, :], bias.partition_broadcast(P)).then_inc(w_in_l, 16)
            for dst, src in ((g1_s, g1), (be1_s, be1), (b1_s, b1), (g2_s, g2), (be2_s, be2), (b2_s, b2)):
                sp.dma_start(dst[:, :], src).then_inc(w_in_l, 16)
            sp.dma_start(nTs[:, :, :], nT.rearrange("p (c j) -> p c j", j=BANK)).then_inc(nT_in, 16)

            def turn(k):
                for s in range(RING):
                    sp.wait_ge(tile_summed, RING * (k - 1) + s + 1)
                    sp.wait_ge(deg_added, RING * (k - 1) + s + 1)
                    load_tile(RING * k + s, s)

            nr_d = n_rows.rearrange("p (c j) -> p c j", j=BANK)
            with sp.Fori(1, TURNS + 1) as k:
                turn(k)
            sp.wait_ge(mh_kept, CHUNKS)
            sp.dma_start(nr[:, 4:CHUNKS, :], nr_d[:, 4:CHUNKS, :]).then_inc(n_in, 16)
            turn(TURNS + 1)
            turn(TURNS + 2)
            sp.wait_ge(xn_made, 3)
            sp.dma_start(nr[:, 4:8, :], nr_d[:, 0:4, :]).then_inc(n_in, 16)
            turn(TURNS + 3)
            turn(TURNS + 4)
            sp.wait_ge(xn_made, 4)
            sp.dma_start(xn_dram.rearrange("p (c j) -> p c j", j=BANK), xr[:, :, :]).then_inc(xn_out, 16)
            with sp.Fori(TURNS + 5, PASS // RING) as k:
                turn(k)
            for s in range(RING):
                sp.wait_ge(tile_summed, PASS - RING + s + 1)
                sp.wait_ge(deg_added, PASS - RING + s + 1)
                load_tile(s, s)
            sp.wait_ge(xn_out, 16)
            sp.wait_ge(z_made, CHUNKS * QT)
            sp.dma_start(x1[:, :, :, :].rearrange("p c i d -> p (c i d)"), xn_dram).then_inc(xn_in, 16)
            with sp.Fori(1, PASS // RING) as k:
                for s in range(RING):
                    sp.wait_ge(split_lo, RING * (k - 1) + s + 1)
                    load_tile(RING * k + s, s)
            with sp.Fori(0, CHUNKS) as c:
                sp.wait_ge(out_made, c + 1)
                sp.dma_start(out_rows.rearrange("p (c i d) -> p c i d", i=CHUNK, d=D)[:, c],
                             x1[:, c]).then_inc(stored, 16)
            sp.wait_ge(stored, 16 * CHUNKS)

        @block.gpsimd
        def _(pool):
            pool.memset(ident[:, :], 0.0).then_inc(const_ok, 1)
            pool.memset(ones[:, :], 1.0).then_inc(const_ok, 1)
            pool.memset(mhalf[:, :], -0.5).then_inc(const_ok, 1)
            pool.wait_ge(const_ok, 3)
            pool.affine_select(out=ident[:, :], in_=ident[:, :], compare_op=ALU.not_equal, fill=1.0,
                               base=0, pattern=[[-1, P]], channel_multiplier=1).then_inc(ident_ok, 1)

            def row_scales(c, var, rstd, shift):
                at4 = cols(CHUNK * c, CHUNK)
                pool.wait_ge(var, c + 1)
                pool.tensor_tensor(ln_rs[:, at4], ln_ve[:, at4], mhalf[:, :], ALU.pow).then_inc(rstd, 1)
                pool.wait_ge(rstd, c + 1)
                pool.tensor_tensor(ln_sh[:, at4], ln_neg[:, at4], ln_rs[:, at4], ALU.mult).then_inc(shift, 1)

            with pool.Fori(0, CHUNKS) as c:
                row_scales(c, ln_var, ln_rstd, ln_shift)

            pool.wait_ge(bn_var, 1)
            pool.tensor_tensor(bn_rs[:, 0:KT], bn_ve[:, 0:KT], mhalf[:, 0:KT], ALU.pow).then_inc(bn_rstd, 1)
            pool.wait_ge(deg_final, 1)
            with pool.Fori(0, CHUNKS) as c:
                at4 = cols(CHUNK * c, CHUNK)
                pool.tensor_tensor(dinv[:, at4], deg[:, at4], mhalf[:, :], ALU.pow).then_inc(pool_step, 1)
            pool.wait_ge(bn_var, 2)
            pool.tensor_tensor(bn_rs[:, :], bn_ve[:, :], mhalf[:, 0:QT], ALU.pow).then_inc(bn_rstd, 1)
            with pool.Fori(0, CHUNKS) as c:
                row_scales(c, ln2_var, ln2_rstd, ln2_shift)
            pool.wait_ge(rows2_norm, CHUNKS * CHUNK)
            with pool.Fori(0, TILES) as t:
                tile = x1[:, :, :, :].rearrange("p c i d -> p (c i) d")[:, cols(t), :]
                pool.tensor_tensor(tile, tile, bias_s[:, :].unsqueeze(1), ALU.add).then_inc(bias_added, 1)

        @block.scalar
        def _(act):
            def normalise(c, rows, shift, done, turned, tiles=CHUNK):
                act.wait_ge(shift, c + 1)
                if turned is not None:
                    act.wait_ge(turned, c)
                for i in range(CHUNK):
                    t = CHUNK * c + i
                    act.activation(hn[:, i, :], rows(c, i), ACT.Relu, bias=ln_sh[:, cols(t)],
                                   scale=ln_rs[:, cols(t)]).then_inc(done, 1)

            def x_tile(c, i):
                return hid[:, cols(c), 1, i * D:(i + 1) * D].squeeze(1)

            def x1_tile(c, i):
                return x1[:, cols(c), i, :].squeeze(1)

            def stage_tile(tile, mt, s, first=False):
                if not first:
                    act.wait_ge(tile_summed, tile - RING + 1)
                act.activation(stage[:, s, :], hid[:, :, 0, :].rearrange("p c (i d) -> p c i d", d=D)[
                    :, cols(mt), s, :].squeeze(1), ACT.Copy).then_inc(staged, 1)

            normalise(0, x_tile, ln_shift, rows_norm, None)
            act.wait_ge(rows_turned, 1)
            normalise(1, x_tile, ln_shift, rows_norm, None)

            def first_turn(k, first=False, ahead=True):
                act.wait_ge(mh_kept, k + 1)
                for s in range(RING):
                    stage_tile(RING * k + s, k, s, first)
                    if s == 1 and ahead:
                        normalise(k + 2, x_tile, ln_shift, rows_norm, rows_turned)

            def keep_group(g):
                act.wait_ge(tile_summed, TILES * (g + 1))
                for j in range(BANKS):
                    act.activation(m2nT[:, bass.ds(GROUP * g + BANK * j, BANK)], acc[:, j, :],
                                   ACT.Copy).then_inc(m2n_kept, 1)

            first_turn(0, first=True)
            with act.Fori(1, TURNS - 2) as k:
                first_turn(k)
            first_turn(TURNS - 2, ahead=False)
            first_turn(TURNS - 1, ahead=False)
            keep_group(0)
            with act.Fori(1, GROUPS) as g:
                with act.Fori(0, TURNS) as k:
                    for s in range(RING):
                        stage_tile(TILES * g + RING * k + s, k, s)
                keep_group(g)

            act.wait_ge(scaled_ok, 1)
            act.wait_ge(nT_in, 16)
            with act.Fori(0, CHUNKS) as c:
                for q in range(QT):
                    act.wait_ge(z_made, QT * c + q + 1)
                    act.activation(hid[:, cols(c), q, :].squeeze(1), ps[q][:, :], ACT.Identity,
                                   bias=c1[:, q:q + 1]).then_inc(z_biased, 1)

            def keep_y(c, first=False):
                act.wait_ge(y_made, c + 1)
                if not first:
                    act.wait_ge(y_turned, c)
                act.activation(yT[:, :], acc[:, 0, :], ACT.Identity, bias=c2[:, 0:1]).then_inc(y_biased, 1)

            def keep_hi(c):
                act.wait_ge(sup_made, c + 1)
                for i in range(CHUNK):
                    act.activation(v2hi[:, cols(c), i * D:(i + 1) * D].squeeze(1),
                                   ps[3][:, i * D:(i + 1) * D], ACT.Copy,
                                   scale=dsc[:, cols(CHUNK * c + i)]).then_inc(hi_kept, 1)

            act.wait_ge(scaled_ok, 2)
            act.wait_ge(d_ok, 1)
            keep_y(0, first=True)
            keep_y(1)
            normalise(0, x1_tile, ln2_shift, rows2_norm, None)
            keep_y(2)
            normalise(1, x1_tile, ln2_shift, rows2_norm, rows2_turned)
            with act.Fori(3, CHUNKS) as c:
                keep_y(c)
                keep_hi(c - 3)
                normalise(c - 1, x1_tile, ln2_shift, rows2_norm, rows2_turned)
            keep_hi(CHUNKS - 3)
            normalise(CHUNKS - 1, x1_tile, ln2_shift, rows2_norm, rows2_turned)
            keep_hi(CHUNKS - 2)
            keep_hi(CHUNKS - 1)

            act.wait_ge(lo_kept, CHUNKS * CHUNK)

            def split_tile(tile, turn, mt, s, first=False):
                if not first:
                    act.wait_ge(tile_summed2, tile - RING + 1)
                act.wait_ge(adj_in[s], 16 * (PASS // RING + turn + 1))
                act.activation(ahi[s], ring[:, s, :].rearrange("p (a b) -> p a b", b=half),
                               ACT.Copy).then_inc(split_hi, 1)
                for part, to in ((v2hi, stage_hi), (v2lo, stage_lo)):
                    act.activation(to[:, s, :], part[:, cols(mt), s * D:(s + 1) * D].squeeze(1).bitcast(F32),
                                   ACT.Copy).then_inc(staged2, 1)

            def keep_sums(g):
                act.wait_ge(tile_summed2, TILES * (g + 1))
                for j in range(BANKS):
                    if not isinstance(g, int) or g:
                        act.wait_ge(sum_turned, BANKS * (g - 1) + j + 1)
                    act.activation(sumT[:, j, :], acc[:, j, :], ACT.Copy).then_inc(sum_kept, 1)

            for s in range(RING):
                split_tile(s, 0, 0, s, first=True)
            with act.Fori(1, TURNS) as k:
                for s in range(RING):
                    split_tile(RING * k + s, k, k, s)
            keep_sums(0)
            with act.Fori(1, GROUPS) as g:
                with act.Fori(0, TURNS) as k:
                    for s in range(RING):
                        split_tile(TILES * g + RING * k + s, TURNS * g + k, k, s)
                keep_sums(g)

        @block.vector
        def _(dve):
            steps = [0]

            def step(ins):
                steps[0] += 1
                ins.then_inc(dve_step, 1)
                dve.wait_ge(dve_step, steps[0])

            def plain():
                dve.wait_ge(const_ok, 3)

            def carry():
                dve.tensor_copy(tick[:, :], ones[:, :])

            def row_stats(c, rows, part, var, first=False):
                plain()
                for i in range(CHUNK):
                    last = dve.bn_stats(ln_bn[:, i, :], rows(c, i))
                last.then_inc(part, 1)
                dve.wait_ge(part, 3 * c + 1)
                carry()
                for i in range(CHUNK):
                    last = dve.bn_aggr(ln_mv[:, i, :], ln_bn[:, i, :])
                last.then_inc(part, 1)
                dve.wait_ge(part, 3 * c + 2)
                at4 = cols(CHUNK * c, CHUNK)
                dve.tensor_scalar(ln_neg[:, at4], ln_mv[:, :, 0], -1.0, None, ALU.mult).then_inc(part, 1)
                dve.tensor_scalar(ln_ve[:, at4], ln_mv[:, :, 1], EPS, None, ALU.add).then_inc(var, 1)
                dve.wait_ge(part, 3 * c + 3)
                dve.wait_ge(var, c + 1)

            def x_tile(c, i):
                return hid[:, cols(c), 1, i * D:(i + 1) * D].squeeze(1)

            def x1_tile(c, i):
                return x1[:, cols(c), i, :].squeeze(1)

            def keep_turned(c):
                dve.wait_ge(rows_turned, c + 1)
                if not isinstance(c, int) or c:
                    dve.wait_ge(mh_made, c)
                dve.tensor_copy(hT[:, :], ps[0][:, :]).then_inc(turned_kept, 1)

            def keep_mh(c):
                dve.wait_ge(mh_made, c + 1)
                dve.tensor_tensor(hid[:, cols(c), 0, :].squeeze(1).rearrange("p (i d) -> p i d", d=D),
                                  ps[1][:, :].rearrange("p (i d) -> p i d", d=D),
                                  b_in_s[:, :].unsqueeze(1).broadcast_to([P, CHUNK, D]),
                                  ALU.add).then_inc(mh_kept, 1)

            def add_tile(tile, turn, s):
                dve.wait_ge(adj_in[s], 16 * (turn + 1))
                if not isinstance(tile, int) or tile:
                    dve.wait_ge(deg_added, tile)
                dve.tensor_tensor(degacc, degacc, ring[:, s, :].rearrange("p (a b) -> p a b", b=BANK),
                                  ALU.add).then_inc(deg_added, 1)

            dve.wait_ge(x_in, 16)
            row_stats(0, x_tile, ln_part, ln_var)
            row_stats(1, x_tile, ln_part, ln_var)
            dve.wait_ge(w_in_l, 16 * 12)
            keep_turned(0)
            keep_mh(0)
            row_stats(2, x_tile, ln_part, ln_var)
            dve.memset(degacc, 0.0).then_inc(deg_clear, 1)
            dve.wait_ge(deg_clear, 1)
            dve.wait_ge(x_in, 32)

            def first_turn(k, make=True, stats=True):
                if make:
                    keep_turned(k + 1)
                for s in range(RING):
                    add_tile(RING * k + s, k, s)
                    if s == 1 and make:
                        keep_mh(k + 1)
                if stats:
                    row_stats(k + 3, x_tile, ln_part, ln_var)

            def end_group(g):
                dve.wait_ge(deg_made, g + 1)
                dve.tensor_copy(deg[:, bass.ds(GROUP // P * g, GROUP // P)],
                                ps[2][:, 0:GROUP // P]).then_inc(deg_kept, 1)
                for j in range(BANKS):
                    plain()
                    dve.wait_ge(m2n_kept, BANKS * g + j + 1)
                    dve.bn_stats(bn1_st[:, 1, bass.ds(BANKS * g + j, 1), :].squeeze(1),
                                 m2nT[:, bass.ds(GROUP * g + BANK * j, BANK)]).then_inc(bn1_seen, 1)

            def clear_degrees(g):
                dve.memset(degacc, 0.0).then_inc(deg_clear, 1)

            first_turn(0)
            with dve.Fori(1, CHUNKS - 3) as k:
                first_turn(k)
            first_turn(CHUNKS - 3, stats=False)
            first_turn(CHUNKS - 2, stats=False)
            first_turn(CHUNKS - 1, make=False, stats=False)
            end_group(0)
            clear_degrees(1)
            dve.wait_ge(nT_in, 16)
            with dve.Fori(0, CHUNKS) as c:
                dve.bn_stats(bn1_st[:, 0, cols(c), :].squeeze(1), nTs[:, cols(c), :].squeeze(1)).then_inc(bn1_seen, 1)
            def add_n(c, src, n):
                dve.tensor_tensor(xr[:, c:c + 4, :], xr[:, c:c + 4, :], nr[:, src:src + 4, :],
                                  ALU.add).then_inc(xn_made, 1)

            def later_turn(g, k):
                dve.wait_ge(deg_clear, g + 1)
                for s in range(RING):
                    add_tile(TILES * g + RING * k + s, TURNS * g + k, s)

            dve.wait_ge(n_in, 16)
            later_turn(1, 0)
            for c in (4, 8, 12):
                add_n(c, c, 1)
            later_turn(1, 1)
            later_turn(1, 2)
            dve.wait_ge(n_in, 32)
            add_n(0, 4, 2)
            with dve.Fori(3, TURNS) as k:
                later_turn(1, k)
            end_group(1)
            with dve.Fori(2, GROUPS) as g:
                clear_degrees(g)
                with dve.Fori(0, TURNS) as k:
                    later_turn(g, k)
                end_group(g)

            def bn_finish(st, n, gamma, beta, tiles):
                for k in range(tiles):
                    last = dve.bn_aggr(bn_mv[:, k, :], st[:, k, :, :].rearrange("p c s -> p (c s)"))
                step(last)
                dve.tensor_scalar(bn_ve[:, 0:tiles], bn_mv[:, 0:tiles, 1], EPS, None, ALU.add).then_inc(bn_var, 1)
                dve.wait_ge(bn_rstd, n)
                step(dve.tensor_tensor(bn_s[:, 0:tiles], bn_rs[:, 0:tiles], gamma[:, :], ALU.mult))
                step(dve.tensor_tensor(bn_ms[:, 0:tiles], bn_mv[:, 0:tiles, 0], bn_s[:, 0:tiles], ALU.mult))
                dve.tensor_tensor(bn_t[:, 0:tiles], beta[:, :], bn_ms[:, 0:tiles], ALU.subtract).then_inc(shift_ok, 1)

            dve.wait_ge(bn1_seen, 2 * CHUNKS)
            bn_finish(bn1_st, 1, g1_s, be1_s, KT)
            dve.wait_ge(cvec_made, 1)
            step(dve.tensor_tensor(c1[:, :], ps[3][:, 0:QT], b1_s[:, :], ALU.add))
            for k in range(KT):
                last = dve.tensor_scalar(w1_s[:, k, :], w1_s[:, k, :], bn_s[:, k:k + 1], None, ALU.mult)
            last.then_inc(scaled_ok, 1)
            dve.wait_ge(deg_kept, GROUPS)
            step(dve.tensor_scalar(dzero[:, :], deg[:, :], 0.0, None, ALU.is_equal))
            dve.tensor_tensor(deg[:, :], deg[:, :], dzero[:, :], ALU.add).then_inc(deg_final, 1)
            dve.wait_ge(pool_step, CHUNKS)
            step(dve.tensor_tensor(dbad[:, :], dinv[:, :], dzero[:, :], ALU.mult))
            dve.tensor_tensor(dsc[:, :], dinv[:, :], dbad[:, :], ALU.subtract).then_inc(d_ok, 1)
            dve.wait_ge(d_ok, 1)

            def leaky(u):
                return dve.scalar_tensor_tensor(out=u, in0=u, scalar=SLOPE, in1=u, op0=ALU.mult, op1=ALU.max)

            with dve.Fori(0, CHUNKS) as c:
                for q in range(QT):
                    dve.wait_ge(z_biased, QT * c + q + 1)
                    leaky(hid[:, cols(c), q, :].squeeze(1)).then_inc(h_kept, 1)
                    plain()
                    dve.wait_ge(h_kept, QT * c + q + 1)
                    dve.bn_stats(bn2_st[:, q, cols(c), :].squeeze(1),
                                 hid[:, cols(c), q, :].squeeze(1)).then_inc(h_seen, 1)
            dve.wait_ge(h_seen, CHUNKS * QT)
            bn_finish(bn2_st, 2, g2_s, be2_s, QT)
            dve.wait_ge(cvec_made, 2)
            step(dve.tensor_tensor(c2[:, :], ps[3][:, 0:1], b2_s[:, :], ALU.add))
            for q in range(QT):
                last = dve.tensor_scalar(w2_s[:, q, :], w2_s[:, q, :], bn_s[:, q:q + 1], None, ALU.mult)
            last.then_inc(scaled_ok, 1)

            def make_x1(c):
                dve.wait_ge(y_biased, c + 1)
                leaky(yT[:, :]).then_inc(y_kept, 1)
                dve.wait_ge(y_turned, c + 1)
                dve.tensor_tensor(x1[:, cols(c), :, :].squeeze(1), x1[:, cols(c), :, :].squeeze(1),
                                  ps[0][:, :].rearrange("p (i d) -> p i d", d=D), ALU.add).then_inc(x1_made, 1)
                plain()
                dve.wait_ge(x1_made, c + 1)
                for i in range(CHUNK):
                    last = dve.bn_stats(ln_bn[:, i, :], x1_tile(c, i))
                last.then_inc(ln_part, 1)
                dve.wait_ge(ln_part, 3 * (CHUNKS + c) + 1)
                carry()
                for i in range(CHUNK):
                    last = dve.bn_aggr(ln_mv[:, i, :], ln_bn[:, i, :])
                last.then_inc(ln_part, 1)
                dve.wait_ge(ln_part, 3 * (CHUNKS + c) + 2)
                at4 = cols(CHUNK * c, CHUNK)
                dve.tensor_scalar(ln_neg[:, at4], ln_mv[:, :, 0], -1.0, None, ALU.mult).then_inc(ln_part, 1)
                dve.tensor_scalar(ln_ve[:, at4], ln_mv[:, :, 1], EPS, None, ALU.add).then_inc(ln2_var, 1)
                dve.wait_ge(ln_part, 3 * (CHUNKS + c) + 3)
                dve.wait_ge(ln2_var, c + 1)

            def keep_turned2(c):
                dve.wait_ge(rows2_turned, c + 1)
                dve.tensor_copy(hT[:, :], ps[1][:, :]).then_inc(turned2_kept, 1)

            def keep_lo(c):
                dve.wait_ge(hi_kept, CHUNK * (c + 1))
                for i in range(CHUNK):
                    dve.scalar_tensor_tensor(
                        out=v2lo[:, cols(c), i * D:(i + 1) * D].squeeze(1),
                        in0=ps[3][:, i * D:(i + 1) * D], scalar=dsc[:, cols(CHUNK * c + i)],
                        in1=v2hi[:, cols(c), i * D:(i + 1) * D].squeeze(1).bitcast(F32),
                        op0=ALU.mult, op1=ALU.subtract).then_inc(lo_kept, 1)

            dve.wait_ge(xn_in, 16)
            make_x1(0)
            make_x1(1)
            keep_turned2(0)
            with dve.Fori(2, CHUNKS) as c:
                make_x1(c)
                keep_lo(c - 2)
                keep_turned2(c - 1)
            keep_lo(CHUNKS - 2)
            keep_turned2(CHUNKS - 1)
            keep_lo(CHUNKS - 1)

            def rest_of_tile(tile, s, first=False):
                dve.wait_ge(split_hi, tile + 1)
                if not first:
                    dve.wait_ge(tile_summed2, tile - RING + 1)
                dve.tensor_tensor(alo[s], ring[:, s, :].rearrange("p (a b) -> p a b", b=half),
                                  ahi[s].bitcast(F32), ALU.subtract).then_inc(split_lo, 1)

            def finish_chunk(c, j):
                dve.wait_ge(sum_turned, c + 1)
                for i in range(CHUNK):
                    last = dve.scalar_tensor_tensor(
                        out=x1_tile(c, i), in0=ps[j][:, i * D:(i + 1) * D], scalar=dsc[:, cols(CHUNK * c + i)],
                        in1=x1_tile(c, i), op0=ALU.mult, op1=ALU.add)
                last.then_inc(out_made, 1)

            for s in range(RING):
                rest_of_tile(s, s, first=True)
            with dve.Fori(1, TURNS) as k:
                for s in range(RING):
                    rest_of_tile(RING * k + s, s)
            dve.wait_ge(bias_added, TILES)
            with dve.Fori(1, GROUPS) as g:
                for s in range(RING):
                    rest_of_tile(TILES * g + s, s)
                    finish_chunk(BANKS * (g - 1) + s, s)
                with dve.Fori(1, TURNS) as k:
                    for s in range(RING):
                        rest_of_tile(TILES * g + RING * k + s, s)
            for j in range(BANKS):
                finish_chunk(BANKS * (GROUPS - 1) + j, j)

        @block.tensor
        def _(pe):
            def turn_rows(c, kept, norm, to, done):
                pe.wait_ge(norm, CHUNK * (c + 1))
                if not isinstance(c, int) or c:
                    pe.wait_ge(kept, c)
                for i in range(CHUNK):
                    last = pe.transpose(to[:, i * D:(i + 1) * D], hn[:, i, :], ident[:, :])
                last.then_inc(done, 1)

            def make_mh(c):
                pe.wait_ge(turned_kept, c + 1)
                if not isinstance(c, int) or c:
                    pe.wait_ge(mh_kept, c)
                for i in range(CHUNK):
                    last = pe.matmul(ps[1][:, i * D:(i + 1) * D], hT[:, i * D:(i + 1) * D], w_in_s[:, :],
                                     start=True, stop=True)
                last.then_inc(mh_made, 1)

            def sum_tile(tile, turn, s, start=False, stop=False, g=0):
                pe.wait_ge(staged, tile + 1)
                pe.wait_ge(adj_in[s], 16 * (turn + 1))
                for j in range(BANKS):
                    if start and g is not None:
                        pe.wait_ge(m2n_kept, BANKS * (g - 1) + j + 1)
                    last = pe.matmul(acc[:, j, :], stage[:, s, :], ring[:, s, j * BANK:(j + 1) * BANK],
                                     start=start, stop=stop)
                last.then_inc(tile_summed, 1)

            pe.wait_ge(ident_ok, 1)
            turn_rows(0, turned_kept, rows_norm, ps[0], rows_turned)
            pe.wait_ge(w_in_l, 16 * 12)
            make_mh(0)

            def first_turn(k, make=True, first=False, end=False):
                if make:
                    turn_rows(k + 1, turned_kept, rows_norm, ps[0], rows_turned)
                for s in range(RING):
                    sum_tile(RING * k + s, k, s, start=first and s == 0, stop=end and s == RING - 1, g=None)
                    if s == 1 and make:
                        make_mh(k + 1)

            def make_degrees(g):
                pe.wait_ge(deg_added, TILES * (g + 1))
                if not isinstance(g, int) or g:
                    pe.wait_ge(deg_kept, g)
                for i in range(GROUP // P):
                    last = pe.matmul(ps[2][:, i:i + 1], degacc[:, i // CHUNK, i % CHUNK * P:(i % CHUNK + 1) * P],
                                     ones[:, :], start=True, stop=True)
                last.then_inc(deg_made, 1)

            def later_turn(g, k, first=False, end=False):
                for s in range(RING):
                    sum_tile(TILES * g + RING * k + s, TURNS * g + k, s, start=first and s == 0,
                             stop=end and s == RING - 1, g=g)

            first_turn(0, first=True)
            with pe.Fori(1, TURNS - 1) as k:
                first_turn(k)
            first_turn(TURNS - 1, make=False, end=True)
            make_degrees(0)
            with pe.Fori(1, GROUPS) as g:
                later_turn(g, 0, first=True)
                with pe.Fori(1, TURNS - 1) as k:
                    later_turn(g, k)
                later_turn(g, TURNS - 1, end=True)
                make_degrees(g)

            pe.wait_ge(shift_ok, 1)
            for q in range(QT):
                for k in range(KT):
                    last = pe.matmul(ps[3][:, q:q + 1], w1_s[:, k, q * P:(q + 1) * P], bn_t[:, k:k + 1],
                                     start=k == 0, stop=k == KT - 1)
            last.then_inc(cvec_made, 1)
            pe.wait_ge(scaled_ok, 1)
            pe.wait_ge(m2n_kept, CHUNKS)

            def make_z(c, first=False):
                for q in range(QT):
                    if not first:
                        pe.wait_ge(z_biased, QT * (c - 1) + q + 1)
                    pe.matmul(ps[q][:, :], w1_s[:, 0, q * P:(q + 1) * P], nTs[:, cols(c), :].squeeze(1),
                              start=True, stop=False)
                    pe.matmul(ps[q][:, :], w1_s[:, 1, q * P:(q + 1) * P], m2nT[:, bass.ds(BANK * c, BANK)],
                              start=False, stop=True).then_inc(z_made, 1)

            make_z(0, first=True)
            with pe.Fori(1, CHUNKS) as c:
                make_z(c)

            pe.wait_ge(shift_ok, 2)
            pe.wait_ge(h_kept, CHUNKS * QT)
            for q in range(QT):
                last = pe.matmul(ps[3][:, 0:1], w2_s[:, q, :], bn_t[:, q:q + 1], start=q == 0, stop=q == QT - 1)
            last.then_inc(cvec_made, 1)
            pe.wait_ge(scaled_ok, 2)

            def make_y(c, first=False):
                if not first:
                    pe.wait_ge(y_biased, c)
                for q in range(QT):
                    last = pe.matmul(acc[:, 0, :], w2_s[:, q, :], hid[:, cols(c), q, :].squeeze(1),
                                     start=q == 0, stop=q == QT - 1)
                last.then_inc(y_made, 1)

            def turn_y(c):
                pe.wait_ge(y_kept, c + 1)
                if not isinstance(c, int) or c:
                    pe.wait_ge(x1_made, c)
                for i in range(CHUNK):
                    last = pe.transpose(ps[0][:, i * D:(i + 1) * D], yT[:, i * P:(i + 1) * P], ident[:, :])
                last.then_inc(y_turned, 1)

            def make_support(c):
                pe.wait_ge(turned2_kept, c + 1)
                if not isinstance(c, int) or c:
                    pe.wait_ge(lo_kept, CHUNK * c)
                for i in range(CHUNK):
                    last = pe.matmul(ps[3][:, i * D:(i + 1) * D], hT[:, i * D:(i + 1) * D], w_s[:, :],
                                     start=True, stop=True)
                last.then_inc(sup_made, 1)

            make_y(0, first=True)
            turn_y(0)
            make_y(1)
            turn_y(1)
            turn_rows(0, turned2_kept, rows2_norm, ps[1], rows2_turned)
            with pe.Fori(2, CHUNKS) as c:
                make_y(c)
                make_support(c - 2)
                turn_y(c)
                turn_rows(c - 1, turned2_kept, rows2_norm, ps[1], rows2_turned)
            make_support(CHUNKS - 2)
            turn_rows(CHUNKS - 1, turned2_kept, rows2_norm, ps[1], rows2_turned)
            make_support(CHUNKS - 1)
            pe.wait_ge(lo_kept, CHUNKS * CHUNK)

            def sum_tile2(tile, s, start=False, stop=False, g=None):
                parts = ((stage_hi, ahi), (stage_hi, alo), (stage_lo, ahi))
                for n, (w, a) in enumerate(parts):
                    if n == 0:
                        pe.wait_ge(staged2, 2 * tile + 2)
                    if n == 1:
                        pe.wait_ge(split_lo, tile + 1)
                    for j in range(BANKS):
                        if start and n == 0 and g is not None:
                            pe.wait_ge(sum_kept, BANKS * (g - 1) + j + 1)
                        last = pe.matmul(acc[:, j, :], w[:, s, :],
                                         a[s][:, j // 2, (j % 2) * BANK:(j % 2 + 1) * BANK],
                                         start=start and n == 0, stop=stop and n == len(parts) - 1)
                last.then_inc(tile_summed2, 1)

            def turn_sums(c, j, first=False):
                pe.wait_ge(sum_kept, c + 1)
                if not first:
                    pe.wait_ge(out_made, c - BANKS + 1)
                for i in range(CHUNK):
                    last = pe.transpose(ps[j][:, i * D:(i + 1) * D], sumT[:, j, i * P:(i + 1) * P], ident[:, :])
                last.then_inc(sum_turned, 1)

            def group2(g, first=False, second=False):
                for s in range(RING):
                    sum_tile2(TILES * g + s, s, start=s == 0, g=None if first else g)
                    if not first:
                        turn_sums(BANKS * (g - 1) + s, s, first=second)
                with pe.Fori(1, TURNS - 1) as k:
                    for s in range(RING):
                        sum_tile2(TILES * g + RING * k + s, s)
                for s in range(RING):
                    sum_tile2(TILES * g + RING * (TURNS - 1) + s, s, stop=s == RING - 1)

            group2(0, first=True)
            group2(1, second=True)
            with pe.Fori(2, GROUPS) as g:
                group2(g)
            for j in range(BANKS):
                turn_sums(BANKS * (GROUPS - 1) + j, j)


def kernel(x, adj, L0_gnn_N, L0_gnn_W_in, L0_gnn_b_in, L0_gnn_g1, L0_gnn_be1, L0_gnn_W1, L0_gnn_b1,
           L0_gnn_g2, L0_gnn_be2, L0_gnn_W2, L0_gnn_b2, L1_gnn_weight, L1_gnn_bias):
    import numpy as np
    import concourse.bacc as bacc
    from concourse.bass_utils import run_bass_kernel_spmd

    def rows(a):
        return np.ascontiguousarray(np.asarray(a).reshape(TILES, P, D).transpose(1, 0, 2).reshape(P, NODES))

    def columns(a):
        return np.ascontiguousarray(np.asarray(a).reshape(-1, P).T)

    adjT = np.ascontiguousarray(
        np.asarray(adj).reshape(GROUPS, GROUP, TILES, P).transpose(0, 2, 3, 1).reshape(GROUPS * TILES, P, GROUP))
    arrays = {
        "adjT": adjT, "x_rows": rows(x), "n_rows": rows(L0_gnn_N),
        "nT": np.ascontiguousarray(np.asarray(L0_gnn_N).T),
        "w_inT": np.ascontiguousarray(np.asarray(L0_gnn_W_in).T), "b_in": np.asarray(L0_gnn_b_in),
        "g1": columns(L0_gnn_g1), "be1": columns(L0_gnn_be1),
        "w1T": np.ascontiguousarray(np.asarray(L0_gnn_W1).T), "b1": columns(L0_gnn_b1),
        "g2": columns(L0_gnn_g2), "be2": columns(L0_gnn_be2),
        "w2T": np.ascontiguousarray(np.asarray(L0_gnn_W2).T), "b2": columns(L0_gnn_b2),
        "weight": np.asarray(L1_gnn_weight), "bias": np.asarray(L1_gnn_bias),
    }
    nc = bacc.Bacc("TRN2", target_bir_lowering=False, num_devices=1, dynamic_dma_scratch_size=SCRATCH)
    args = [nc.dram_tensor(name, a.shape, F32, kind="ExternalInput").ap() for name, a in arrays.items()]
    out_rows = nc.dram_tensor("out_rows", (P, NODES), F32, kind="ExternalOutput").ap()
    xn_dram = nc.dram_tensor("xn_dram", (P, NODES), F32, kind="Internal").ap()
    gnn_kernel(nc, *args, out_rows, xn_dram)
    result = run_bass_kernel_spmd(nc, [arrays], core_ids=[0])
    got = result.results[0]["out_rows"]
    return got.reshape(P, TILES, D).transpose(1, 0, 2).reshape(NODES, D)
```

```python
from contextlib import ExitStack

import concourse.bass as bass
from concourse import mybir

F32 = mybir.dt.float32
F32R = mybir.dt.float32r
ALU = mybir.AluOpType
ACT = mybir.ActivationFunctionType

P = 128
D = 128
NODES = 8192
H = 512
EPS = 1e-5
SLOPE = 0.01

BANK = 512
GROUP = 2048
GROUPS = NODES // GROUP
BANKS = GROUP // BANK
TILES = NODES // P
CHUNK = BANK // P
CHUNKS = NODES // BANK
RING = 4
TURNS = TILES // RING
KT = 2 * D // P
QT = H // P
HALF = GROUP // 2
HALVES = 2
PAIRS = 4
SPLIT = (1,)
SCRATCH = 1024


def gnn_kernel(nc, adjT, x_rows, n_rows, nT, w_inT, b_in, g1, be1, w1T, b1, g2, be2, w2T, b2,
               weight, bias, out_rows):
    with ExitStack() as ctx:
        top = [-(-nc.sbuf_base // 64) * 64]

        def at(name, shape, dt=F32, offset=None):
            size = 4
            for n in shape[1:]:
                size *= n
            if offset is None:
                offset = top[0]
                top[0] += -(-size // 32) * 32
            return nc.alloc_sbuf_tensor_at(name, shape, dt, offset=offset)

        ring = at("ring", [P, RING, GROUP])
        m2n_base = top[0]
        m2nT = at("m2nT", [P, NODES])
        halves = at("halves", [P, PAIRS, 2, 2, BANK], F32R, offset=m2n_base)
        space = top[0]
        hid = at("hid", [P, CHUNKS, QT, BANK])
        parts = at("parts", [P, CHUNKS, QT, BANK], F32R, offset=space)
        xr = hid[:, :, 1, :]
        nTs = hid[:, :, 3, :]
        degacc = [hid[:, 4 * b:4 * b + 4, 2, :] for b in range(2)]
        first_halves = [[parts[:, 8 + 4 * b + 2 * n:10 + 4 * b + 2 * n, 2, :] for n in range(2)]
                        for b in range(2)]
        sumT = hid[:, 0:BANKS, 3, :]

        def x1_chunk(c):
            return hid[:, bass.ds(c, 1), 2, :].squeeze(1)

        def x1_tile(c, i):
            return hid[:, bass.ds(c, 1), 2, i * D:(i + 1) * D].squeeze(1)

        def x_tile(c, i):
            return hid[:, bass.ds(c, 1), 1, i * D:(i + 1) * D].squeeze(1)

        def ring_half(s, h):
            return ring[:, s, h * HALF:(h + 1) * HALF].rearrange("p (a b) -> p a b", b=BANK)

        work = top[0]
        stage = at("stage", [P, RING, D])
        stage_lo1 = at("stage_lo1", [P, RING, D], F32R)
        stage_hi = at("stage_hi", [P, RING, D], F32R)
        stage_lo = at("stage_lo", [P, RING, D], F32R, offset=work)
        hn = at("hn", [P, CHUNK, D])
        hT = at("hT", [P, BANK])
        yT = at("yT", [P, BANK])

        w_in_s = at("w_in_s", [P, D])
        w1_s = at("w1_s", [P, KT, H])
        w2_s = at("w2_s", [P, QT, D])
        w_s = at("w_s", [P, D])
        ident = at("ident", [P, P])
        b_in_s = at("b_in_s", [P, D])
        bias_s = at("bias_s", [P, D])
        g1_s = at("g1_s", [P, KT])
        be1_s = at("be1_s", [P, KT])
        b1_s = at("b1_s", [P, QT])
        g2_s = at("g2_s", [P, QT])
        be2_s = at("be2_s", [P, QT])
        b2_s = at("b2_s", [P, 1])
        ones = at("ones", [P, 1])
        mhalf = at("mhalf", [P, CHUNK])
        ln_bn = at("ln_bn", [P, CHUNK, 6])
        ln_mv = at("ln_mv", [P, CHUNK, 2])
        ln_neg = at("ln_neg", [P, TILES])
        ln_ve = at("ln_ve", [P, TILES])
        ln_rs = at("ln_rs", [P, TILES])
        ln_sh = at("ln_sh", [P, TILES])
        bn1_st = at("bn1_st", [P, KT, CHUNKS, 6])
        bn2_st = at("bn2_st", [P, QT, CHUNKS, 6])
        bn_mv = at("bn_mv", [P, QT, 2])
        bn_ve = at("bn_ve", [P, QT])
        bn_rs = at("bn_rs", [P, QT])
        bn_s = at("bn_s", [P, QT])
        bn_ms = at("bn_ms", [P, QT])
        bn_t = at("bn_t", [P, QT])
        c1 = at("c1", [P, QT])
        c2 = at("c2", [P, 1])
        tick = at("tick", [P, 1])
        deg = at("deg", [P, TILES])
        dzero = at("dzero", [P, TILES])
        dinv = at("dinv", [P, TILES])
        dbad = at("dbad", [P, TILES])
        dsc = at("dsc", [P, TILES])
        assert top[0] <= nc.sbuf_top, top[0]

        acc = ctx.enter_context(nc.psum_tensor("acc", [P, BANKS, BANK], F32))
        ps = [ctx.enter_context(nc.psum_tensor(f"ps{i}", [P, BANK], F32)) for i in range(4)]

        def sem(name):
            return ctx.enter_context(nc.semaphore(name))

        x_in, win_in, nT_in, w_in_l, xn_in, stored = (
            sem(n) for n in ("x_in", "win_in", "nT_in", "w_in_l", "xn_in", "stored"))
        adj_in = [sem(f"adj_in{s}") for s in range(RING)]
        const_ok, ident_ok = sem("const_ok"), sem("ident_ok")
        ln_part, ln_var, ln_rstd, ln_shift = sem("ln_part"), sem("ln_var"), sem("ln_rstd"), sem("ln_shift")
        rows_norm, rows_turned, turned_kept, mh_made, mh_kept = (
            sem(n) for n in ("rows_norm", "rows_turned", "turned_kept", "mh_made", "mh_kept"))
        staged, tile_summed, deg_added = sem("staged"), sem("tile_summed"), sem("deg_added")
        hi_staged, lo_staged, hi_split, lo_split = (
            sem(n) for n in ("hi_staged", "lo_staged", "hi_split", "lo_split"))
        m2n_kept, deg_made, deg_kept, bn1_seen = (
            sem(n) for n in ("m2n_kept", "deg_made", "deg_kept", "bn1_seen"))
        xn_made = sem("xn_made")
        dve_step, pool_step = sem("dve_step"), sem("pool_step")
        bn_var, bn_rstd, shift_ok, cvec_made, scaled_ok = (
            sem(n) for n in ("bn_var", "bn_rstd", "shift_ok", "cvec_made", "scaled_ok"))
        z_made, z_biased, h_kept, h_seen = sem("z_made"), sem("z_biased"), sem("h_kept"), sem("h_seen")
        y_made, y_biased, y_kept, y_turned, x1_made = sem("y_made"), sem("y_biased"), sem("y_kept"), sem("y_turned"), sem("x1_made")
        deg_final, d_ok = sem("deg_final"), sem("d_ok")
        ln2_var, ln2_rstd, ln2_shift = sem("ln2_var"), sem("ln2_rstd"), sem("ln2_shift")
        rows2_norm, rows2_turned, turned2_kept, sup_made, hi_kept, lo_kept = (
            sem(n) for n in ("rows2_norm", "rows2_turned", "turned2_kept", "sup_made", "hi_kept", "lo_kept"))
        bias_added = sem("bias_added")
        staged2, split_hi, split_lo, half_summed = (
            sem(n) for n in ("staged2", "split_hi", "split_lo", "half_summed"))
        sum_kept, sum_turned, out_made = sem("sum_kept"), sem("sum_turned"), sem("out_made")

        PASS = GROUPS * TILES

        def cols(t, n=1):
            return bass.ds(t, n)

        block = ctx.enter_context(nc.Block())

        @block.sync
        def _(sp):
            xr_d = x_rows.rearrange("p (c j) -> p c j", j=BANK)
            sp.dma_start(xr[:, 0:4, :], xr_d[:, 0:4, :]).then_inc(x_in, 16)
            sp.dma_start(w_in_s[:, :], w_inT).then_inc(win_in, 16)
            sp.dma_start(b_in_s[:, :], b_in.partition_broadcast(P)).then_inc(win_in, 16)

            def load_tile(tile, s):
                sp.dma_start(ring[:, s, :], adjT[tile]).then_inc(adj_in[s], 16)

            for s in range(RING):
                load_tile(s, s)
                if s == 1:
                    sp.wait_ge(x_in, 16)
                    sp.dma_start(xr[:, 4:CHUNKS, :], xr_d[:, 4:CHUNKS, :]).then_inc(x_in, 16)
            sp.dma_start(w1_s[:, :, :], w1T.rearrange("(k p) h -> p k h", p=P)).then_inc(w_in_l, 16)
            sp.dma_start(w2_s[:, :, :], w2T.rearrange("(k p) h -> p k h", p=P)).then_inc(w_in_l, 16)
            sp.dma_start(w_s[:, :], weight).then_inc(w_in_l, 16)
            sp.dma_start(bias_s[:, :], bias.partition_broadcast(P)).then_inc(w_in_l, 16)
            for dst, src in ((g1_s, g1), (be1_s, be1), (b1_s, b1), (g2_s, g2), (be2_s, be2), (b2_s, b2)):
                sp.dma_start(dst[:, :], src).then_inc(w_in_l, 16)
            sp.dma_start(nTs[:, :, :], nT.rearrange("p (c j) -> p c j", j=BANK)).then_inc(nT_in, 16)

            with sp.Fori(1, PASS // RING) as k:
                for s in range(RING):
                    sp.wait_ge(tile_summed, RING * (k - 1) + s + 1)
                    sp.wait_ge(deg_added, RING * (k - 1) + s + 1)
                    load_tile(RING * k + s, s)
            for s in range(RING):
                sp.wait_ge(tile_summed, PASS - RING + s + 1)
                sp.wait_ge(deg_added, PASS - RING + s + 1)
                load_tile(s, s)
            with sp.Fori(1, PASS // RING) as k:
                for s in range(RING):
                    sp.wait_ge(split_lo, HALVES * (RING * (k - 1) + s + 1))
                    load_tile(RING * k + s, s)
            with sp.Fori(0, CHUNKS) as c:
                sp.wait_ge(out_made, c + 1)
                sp.dma_start(out_rows.rearrange("p (c j) -> p c j", j=BANK)[:, bass.ds(c, 1), :].squeeze(1),
                             x1_chunk(c)).then_inc(stored, 16)
            sp.wait_ge(stored, 16 * CHUNKS)

        @block.gpsimd
        def _(pool):
            pool.memset(ident[:, :], 0.0).then_inc(const_ok, 1)
            pool.memset(ones[:, :], 1.0).then_inc(const_ok, 1)
            pool.memset(mhalf[:, :], -0.5).then_inc(const_ok, 1)
            pool.wait_ge(const_ok, 3)
            pool.affine_select(out=ident[:, :], in_=ident[:, :], compare_op=ALU.not_equal, fill=1.0,
                               base=0, pattern=[[-1, P]], channel_multiplier=1).then_inc(ident_ok, 1)

            def row_scales(c, var, rstd, shift):
                at4 = cols(CHUNK * c, CHUNK)
                pool.wait_ge(var, c + 1)
                pool.tensor_tensor(ln_rs[:, at4], ln_ve[:, at4], mhalf[:, :], ALU.pow).then_inc(rstd, 1)
                pool.wait_ge(rstd, c + 1)
                pool.tensor_tensor(ln_sh[:, at4], ln_neg[:, at4], ln_rs[:, at4], ALU.mult).then_inc(shift, 1)

            with pool.Fori(0, CHUNKS) as c:
                row_scales(c, ln_var, ln_rstd, ln_shift)

            pool.wait_ge(bn_var, 1)
            pool.tensor_tensor(bn_rs[:, 0:KT], bn_ve[:, 0:KT], mhalf[:, 0:KT], ALU.pow).then_inc(bn_rstd, 1)
            pool.wait_ge(deg_final, 1)
            with pool.Fori(0, CHUNKS) as c:
                at4 = cols(CHUNK * c, CHUNK)
                pool.tensor_tensor(dinv[:, at4], deg[:, at4], mhalf[:, :], ALU.pow).then_inc(pool_step, 1)
            pool.wait_ge(bn_var, 2)
            pool.tensor_tensor(bn_rs[:, :], bn_ve[:, :], mhalf[:, 0:QT], ALU.pow).then_inc(bn_rstd, 1)
            def add_rows(c):
                pool.wait_ge(xn_in, 32 * (c + 1))
                pool.tensor_tensor(x1_chunk(c), x1_chunk(c), hid[:, cols(c), 3, :].squeeze(1),
                                   ALU.add).then_inc(xn_made, 1)

            add_rows(0)
            add_rows(1)
            row_scales(0, ln2_var, ln2_rstd, ln2_shift)
            with pool.Fori(2, CHUNKS) as c:
                add_rows(c)
                row_scales(c - 1, ln2_var, ln2_rstd, ln2_shift)
            row_scales(CHUNKS - 1, ln2_var, ln2_rstd, ln2_shift)
            pool.wait_ge(rows2_norm, CHUNKS * CHUNK)
            with pool.Fori(0, CHUNKS) as c:
                for i in range(CHUNK):
                    pool.tensor_tensor(x1_tile(c, i), x1_tile(c, i), bias_s[:, :], ALU.add).then_inc(bias_added, 1)

        @block.scalar
        def _(act):
            def normalise(c, rows, shift, done, turned, tiles=CHUNK):
                act.wait_ge(shift, c + 1)
                if turned is not None:
                    act.wait_ge(turned, c)
                for i in range(CHUNK):
                    t = CHUNK * c + i
                    act.activation(hn[:, i, :], rows(c, i), ACT.Relu, bias=ln_sh[:, cols(t)],
                                   scale=ln_rs[:, cols(t)]).then_inc(done, 1)

            def mh_tile(t, s):
                return hid[:, cols(t), 0, s * D:(s + 1) * D].squeeze(1)

            def feed_tile(g, k, s, first=False):
                tile = TILES * g + RING * k + s
                if not first:
                    act.wait_ge(tile_summed, tile - RING + 1)
                if s not in SPLIT:
                    act.activation(stage[:, s, :], mh_tile(k, s), ACT.Copy).then_inc(staged, 1)
                    return
                act.activation(stage_hi[:, s, :], mh_tile(k, s), ACT.Copy).then_inc(hi_staged, 1)
                act.wait_ge(adj_in[s], 16 * (TURNS * g + k + 1))
                for h in range(HALVES):
                    act.activation(first_halves[h][0], ring_half(s, h), ACT.Copy).then_inc(hi_split, 1)

            def first_turn(k, first=False, ahead=True):
                act.wait_ge(mh_kept, k + 1)
                for s in range(RING):
                    feed_tile(0, k, s, first)
                    if s == 2 and ahead:
                        normalise(k + 2, x_tile, ln_shift, rows_norm, rows_turned)

            def keep_group(g):
                act.wait_ge(tile_summed, TILES * (g + 1))
                for j in range(BANKS):
                    act.activation(m2nT[:, bass.ds(GROUP * g + BANK * j, BANK)], acc[:, j, :],
                                   ACT.Copy).then_inc(m2n_kept, 1)

            normalise(0, x_tile, ln_shift, rows_norm, None)
            act.wait_ge(rows_turned, 1)
            normalise(1, x_tile, ln_shift, rows_norm, None)
            first_turn(0, first=True)
            with act.Fori(1, TURNS - 2) as k:
                first_turn(k)
            first_turn(TURNS - 2, ahead=False)
            first_turn(TURNS - 1, ahead=False)
            for g in range(1, GROUPS):
                feed_tile(g, 0, 0)
                keep_group(g - 1)
                for s in range(1, RING):
                    feed_tile(g, 0, s)
                with act.Fori(1, TURNS) as k:
                    for s in range(RING):
                        feed_tile(g, k, s)
            keep_group(GROUPS - 1)

            act.wait_ge(scaled_ok, 1)
            act.wait_ge(nT_in, 16)
            with act.Fori(0, CHUNKS) as c:
                for q in range(QT):
                    act.wait_ge(z_made, QT * c + q + 1)
                    act.activation(hid[:, cols(c), q, :].squeeze(1), ps[q][:, :], ACT.Identity,
                                   bias=c1[:, q:q + 1]).then_inc(z_biased, 1)

            def keep_y(c, first=False):
                act.wait_ge(y_made, c + 1)
                if not first:
                    act.wait_ge(y_turned, c)
                act.activation(yT[:, :], ps[2][:, :], ACT.Identity, bias=c2[:, 0:1]).then_inc(y_biased, 1)
                if not first:
                    act.wait_ge(xn_made, c)
                act.dma_start(x1_chunk(c), x_rows.rearrange("p (c j) -> p c j", j=BANK)[
                    :, cols(c), :].squeeze(1)).then_inc(xn_in, 16)
                act.dma_start(hid[:, cols(c), 3, :].squeeze(1), n_rows.rearrange("p (c j) -> p c j", j=BANK)[
                    :, cols(c), :].squeeze(1)).then_inc(xn_in, 16)

            def keep_hi(c):
                act.wait_ge(sup_made, c + 1)
                for i in range(CHUNK):
                    act.activation(parts[:, cols(c), 0, i * D:(i + 1) * D].squeeze(1),
                                   ps[3][:, i * D:(i + 1) * D], ACT.Copy,
                                   scale=dsc[:, cols(CHUNK * c + i)]).then_inc(hi_kept, 1)

            act.wait_ge(scaled_ok, 2)
            act.wait_ge(d_ok, 1)
            keep_y(0, first=True)
            keep_y(1)
            normalise(0, x1_tile, ln2_shift, rows2_norm, None)
            keep_y(2)
            keep_hi(0)
            normalise(1, x1_tile, ln2_shift, rows2_norm, rows2_turned)

            def split_tile(g, k, s, first=False):
                tile = TILES * g + RING * k + s
                if not first:
                    act.wait_ge(half_summed, HALVES * (tile - RING + 1))
                for n, to in enumerate((stage_hi, stage_lo)):
                    act.activation(to[:, s, :], parts[:, cols(k), n, s * D:(s + 1) * D].squeeze(1).bitcast(F32),
                                   ACT.Copy).then_inc(staged2, 1)
                act.wait_ge(adj_in[s], 16 * (TURNS * (GROUPS + g) + k + 1))
                for h in range(HALVES):
                    pair = HALVES * (s % 2) + h
                    if not (first and s < 2):
                        act.wait_ge(half_summed, HALVES * tile + h - PAIRS + 1)
                    act.activation(halves[:, pair, 0], ring_half(s, h), ACT.Copy).then_inc(split_hi, 1)

            def made_turn(k, first=False, y=True, norm=True, support=True):
                act.wait_ge(lo_kept, CHUNK * (k + 1))
                split_tile(0, k, 0, first)
                split_tile(0, k, 1, first)
                if y:
                    keep_y(k + 3)
                split_tile(0, k, 2, first)
                if support:
                    keep_hi(k + 1)
                split_tile(0, k, 3, first)
                if norm:
                    normalise(k + 2, x1_tile, ln2_shift, rows2_norm, rows2_turned)

            made_turn(0, first=True)
            with act.Fori(1, TURNS - 3) as k:
                made_turn(k)
            made_turn(TURNS - 3, y=False)
            made_turn(TURNS - 2, y=False, norm=False)
            made_turn(TURNS - 1, y=False, norm=False, support=False)

            def keep_sums(g):
                act.wait_ge(half_summed, HALVES * TILES * (g + 1))
                for j in range(BANKS):
                    if g:
                        act.wait_ge(sum_turned, BANKS * (g - 1) + j + 1)
                    act.activation(sumT[:, j, :], acc[:, j, :], ACT.Copy).then_inc(sum_kept, 1)

            for g in range(1, GROUPS):
                split_tile(g, 0, 0)
                keep_sums(g - 1)
                for s in range(1, RING):
                    split_tile(g, 0, s)
                with act.Fori(1, TURNS) as k:
                    for s in range(RING):
                        split_tile(g, k, s)
            keep_sums(GROUPS - 1)

        @block.vector
        def _(dve):
            steps = [0]

            def step(ins):
                steps[0] += 1
                ins.then_inc(dve_step, 1)
                dve.wait_ge(dve_step, steps[0])

            def plain():
                dve.wait_ge(const_ok, 3)

            def carry():
                dve.tensor_copy(tick[:, :], ones[:, :])

            def row_stats(c, rows, part, var, first=False):
                plain()
                for i in range(CHUNK):
                    last = dve.bn_stats(ln_bn[:, i, :], rows(c, i))
                last.then_inc(part, 1)
                dve.wait_ge(part, 3 * c + 1)
                carry()
                for i in range(CHUNK):
                    last = dve.bn_aggr(ln_mv[:, i, :], ln_bn[:, i, :])
                last.then_inc(part, 1)
                dve.wait_ge(part, 3 * c + 2)
                at4 = cols(CHUNK * c, CHUNK)
                dve.tensor_scalar(ln_neg[:, at4], ln_mv[:, :, 0], -1.0, None, ALU.mult).then_inc(part, 1)
                dve.tensor_scalar(ln_ve[:, at4], ln_mv[:, :, 1], EPS, None, ALU.add).then_inc(var, 1)
                dve.wait_ge(part, 3 * c + 3)
                dve.wait_ge(var, c + 1)

            def keep_turned(c):
                dve.wait_ge(rows_turned, c + 1)
                if not isinstance(c, int) or c:
                    dve.wait_ge(mh_made, c)
                dve.tensor_copy(hT[:, :], ps[0][:, :]).then_inc(turned_kept, 1)

            def keep_mh(c):
                dve.wait_ge(mh_made, c + 1)
                dve.tensor_tensor(hid[:, cols(c), 0, :].squeeze(1).rearrange("p (i d) -> p i d", d=D),
                                  ps[1][:, :].rearrange("p (i d) -> p i d", d=D),
                                  b_in_s[:, :].unsqueeze(1).broadcast_to([P, CHUNK, D]),
                                  ALU.add).then_inc(mh_kept, 1)

            def add_tile(g, k, s):
                tile, sums = TILES * g + RING * k + s, degacc[g % 2]
                dve.wait_ge(adj_in[s], 16 * (TURNS * g + k + 1))
                if isinstance(k, int) and k == 0 and s == 0:
                    if g >= 2:
                        dve.wait_ge(deg_made, g - 1)
                    dve.tensor_copy(sums, ring[:, s, :].rearrange("p (a b) -> p a b", b=BANK)).then_inc(deg_added, 1)
                else:
                    if s in SPLIT:
                        dve.wait_ge(hi_staged, TURNS * g + k + 1)
                        dve.tensor_tensor(stage_lo1[:, s, :], hid[:, cols(k), 0, s * D:(s + 1) * D].squeeze(1),
                                          stage_hi[:, s, :].bitcast(F32), ALU.subtract).then_inc(lo_staged, 1)
                        for h in range(HALVES):
                            dve.wait_ge(hi_split, HALVES * (TURNS * g + k) + h + 1)
                            dve.tensor_tensor(first_halves[h][1], ring_half(s, h),
                                              first_halves[h][0].bitcast(F32), ALU.subtract).then_inc(lo_split, 1)
                    dve.wait_ge(deg_added, tile)
                    dve.tensor_tensor(sums, sums, ring[:, s, :].rearrange("p (a b) -> p a b", b=BANK),
                                      ALU.add).then_inc(deg_added, 1)

            dve.wait_ge(x_in, 16)
            row_stats(0, x_tile, ln_part, ln_var)
            row_stats(1, x_tile, ln_part, ln_var)
            dve.wait_ge(win_in, 32)
            keep_turned(0)
            keep_mh(0)
            row_stats(2, x_tile, ln_part, ln_var)

            def first_turn(k, make=True, stats=True):
                if make:
                    keep_turned(k + 1)
                for s in range(RING):
                    add_tile(0, k, s)
                    if s == 1 and make:
                        keep_mh(k + 1)
                if stats:
                    row_stats(k + 3, x_tile, ln_part, ln_var)

            def end_group(g):
                dve.wait_ge(deg_made, g + 1)
                dve.tensor_copy(deg[:, bass.ds(GROUP // P * g, GROUP // P)],
                                ps[2][:, 0:GROUP // P]).then_inc(deg_kept, 1)
                for j in range(BANKS):
                    dve.wait_ge(m2n_kept, BANKS * g + j + 1)
                    dve.bn_stats(bn1_st[:, 1, BANKS * g + j, :],
                                 m2nT[:, bass.ds(GROUP * g + BANK * j, BANK)]).then_inc(bn1_seen, 1)

            def nT_stats(c):
                dve.bn_stats(bn1_st[:, 0, c, :], nTs[:, c, :]).then_inc(bn1_seen, 1)

            first_turn(0)
            dve.wait_ge(x_in, 32)
            with dve.Fori(1, CHUNKS - 3) as k:
                first_turn(k)
            first_turn(CHUNKS - 3, stats=False)
            first_turn(CHUNKS - 2, stats=False)
            first_turn(CHUNKS - 1, make=False, stats=False)
            dve.wait_ge(nT_in, 16)
            for g in range(1, GROUPS):
                for s in range(RING):
                    add_tile(g, 0, s)
                    if s == 1:
                        end_group(g - 1)
                for k in range(1, 1 + CHUNKS // 2):
                    for s in range(RING):
                        add_tile(g, k, s)
                    if g < 3:
                        nT_stats(CHUNKS // 2 * (g - 1) + k - 1)
                with dve.Fori(1 + CHUNKS // 2, TURNS) as k:
                    for s in range(RING):
                        add_tile(g, k, s)
            end_group(GROUPS - 1)

            def bn_finish(st, n, gamma, beta, tiles):
                for k in range(tiles):
                    last = dve.bn_aggr(bn_mv[:, k, :], st[:, k, :, :].rearrange("p c s -> p (c s)"))
                step(last)
                dve.tensor_scalar(bn_ve[:, 0:tiles], bn_mv[:, 0:tiles, 1], EPS, None, ALU.add).then_inc(bn_var, 1)
                dve.wait_ge(bn_rstd, n)
                step(dve.tensor_tensor(bn_s[:, 0:tiles], bn_rs[:, 0:tiles], gamma[:, :], ALU.mult))
                step(dve.tensor_tensor(bn_ms[:, 0:tiles], bn_mv[:, 0:tiles, 0], bn_s[:, 0:tiles], ALU.mult))
                dve.tensor_tensor(bn_t[:, 0:tiles], beta[:, :], bn_ms[:, 0:tiles], ALU.subtract).then_inc(shift_ok, 1)

            dve.wait_ge(bn1_seen, 2 * CHUNKS)
            bn_finish(bn1_st, 1, g1_s, be1_s, KT)
            dve.wait_ge(cvec_made, 1)
            step(dve.tensor_tensor(c1[:, :], ps[3][:, 0:QT], b1_s[:, :], ALU.add))
            for k in range(KT):
                last = dve.tensor_scalar(w1_s[:, k, :], w1_s[:, k, :], bn_s[:, k:k + 1], None, ALU.mult)
            last.then_inc(scaled_ok, 1)
            dve.wait_ge(deg_kept, GROUPS)
            step(dve.tensor_scalar(dzero[:, :], deg[:, :], 0.0, None, ALU.is_equal))
            dve.tensor_tensor(deg[:, :], deg[:, :], dzero[:, :], ALU.add).then_inc(deg_final, 1)
            dve.wait_ge(pool_step, CHUNKS)
            step(dve.tensor_tensor(dbad[:, :], dinv[:, :], dzero[:, :], ALU.mult))
            dve.tensor_tensor(dsc[:, :], dinv[:, :], dbad[:, :], ALU.subtract).then_inc(d_ok, 1)
            dve.wait_ge(d_ok, 1)

            def leaky(u):
                return dve.scalar_tensor_tensor(out=u, in0=u, scalar=SLOPE, in1=u, op0=ALU.mult, op1=ALU.max)

            with dve.Fori(0, CHUNKS) as c:
                for q in range(QT):
                    dve.wait_ge(z_biased, QT * c + q + 1)
                    leaky(hid[:, cols(c), q, :].squeeze(1)).then_inc(h_kept, 1)
                    plain()
                    dve.wait_ge(h_kept, QT * c + q + 1)
                    dve.bn_stats(bn2_st[:, q, cols(c), :].squeeze(1),
                                 hid[:, cols(c), q, :].squeeze(1)).then_inc(h_seen, 1)
            dve.wait_ge(h_seen, CHUNKS * QT)
            bn_finish(bn2_st, 2, g2_s, be2_s, QT)
            dve.wait_ge(cvec_made, 2)
            step(dve.tensor_tensor(c2[:, :], ps[3][:, 0:1], b2_s[:, :], ALU.add))
            for q in range(QT):
                last = dve.tensor_scalar(w2_s[:, q, :], w2_s[:, q, :], bn_s[:, q:q + 1], None, ALU.mult)
            last.then_inc(scaled_ok, 1)

            def leave_y(c):
                dve.wait_ge(y_biased, c + 1)
                leaky(yT[:, :]).then_inc(y_kept, 1)

            def make_x1(c):
                dve.wait_ge(xn_made, c + 1)
                dve.wait_ge(y_turned, c + 1)
                dve.tensor_tensor(x1_chunk(c), x1_chunk(c), ps[0][:, :], ALU.add).then_inc(x1_made, 1)
                plain()
                dve.wait_ge(x1_made, c + 1)
                for i in range(CHUNK):
                    last = dve.bn_stats(ln_bn[:, i, :], x1_tile(c, i))
                last.then_inc(ln_part, 1)
                dve.wait_ge(ln_part, 3 * (CHUNKS + c) + 1)
                carry()
                for i in range(CHUNK):
                    last = dve.bn_aggr(ln_mv[:, i, :], ln_bn[:, i, :])
                last.then_inc(ln_part, 1)
                dve.wait_ge(ln_part, 3 * (CHUNKS + c) + 2)
                at4 = cols(CHUNK * c, CHUNK)
                dve.tensor_scalar(ln_neg[:, at4], ln_mv[:, :, 0], -1.0, None, ALU.mult).then_inc(ln_part, 1)
                dve.tensor_scalar(ln_ve[:, at4], ln_mv[:, :, 1], EPS, None, ALU.add).then_inc(ln2_var, 1)
                dve.wait_ge(ln_part, 3 * (CHUNKS + c) + 3)
                dve.wait_ge(ln2_var, c + 1)

            def keep_turned2(c):
                dve.wait_ge(rows2_turned, c + 1)
                if not isinstance(c, int) or c:
                    dve.wait_ge(sup_made, c)
                dve.tensor_copy(hT[:, :], ps[1][:, :]).then_inc(turned2_kept, 1)

            def keep_lo(c):
                dve.wait_ge(hi_kept, CHUNK * (c + 1))
                for i in range(CHUNK):
                    dve.scalar_tensor_tensor(
                        out=parts[:, cols(c), 1, i * D:(i + 1) * D].squeeze(1),
                        in0=ps[3][:, i * D:(i + 1) * D], scalar=dsc[:, cols(CHUNK * c + i)],
                        in1=parts[:, cols(c), 0, i * D:(i + 1) * D].squeeze(1).bitcast(F32),
                        op0=ALU.mult, op1=ALU.subtract).then_inc(lo_kept, 1)

            leave_y(0)
            make_x1(0)
            leave_y(1)
            make_x1(1)
            keep_turned2(0)
            leave_y(2)
            keep_lo(0)

            def rest_of_tile(g, k, s):
                tile = TILES * g + RING * k + s
                for h in range(HALVES):
                    pair = HALVES * (s % 2) + h
                    dve.wait_ge(split_hi, HALVES * tile + h + 1)
                    dve.tensor_tensor(halves[:, pair, 1], ring_half(s, h),
                                      halves[:, pair, 0].bitcast(F32), ALU.subtract).then_inc(split_lo, 1)

            def made_turn(k, y=True, x1=True, support=True):
                rest_of_tile(0, k, 0)
                if support:
                    keep_turned2(k + 1)
                rest_of_tile(0, k, 1)
                if x1:
                    make_x1(k + 2)
                rest_of_tile(0, k, 2)
                if y:
                    leave_y(k + 3)
                rest_of_tile(0, k, 3)
                if support:
                    keep_lo(k + 1)

            def finish_chunk(c, j):
                dve.wait_ge(sum_turned, c + 1)
                for i in range(CHUNK):
                    last = dve.scalar_tensor_tensor(
                        out=x1_tile(c, i), in0=ps[j][:, i * D:(i + 1) * D], scalar=dsc[:, cols(CHUNK * c + i)],
                        in1=x1_tile(c, i), op0=ALU.mult, op1=ALU.add)
                last.then_inc(out_made, 1)

            with dve.Fori(0, TURNS - 3) as k:
                made_turn(k)
            made_turn(TURNS - 3, y=False)
            made_turn(TURNS - 2, y=False, x1=False)
            made_turn(TURNS - 1, y=False, x1=False, support=False)
            for g in range(1, GROUPS):
                rest_of_tile(g, 0, 0)
                rest_of_tile(g, 0, 1)
                if g == 1:
                    dve.wait_ge(bias_added, TILES)
                for s in range(RING):
                    rest_of_tile(g, (s + 2) // RING, (s + 2) % RING)
                    finish_chunk(BANKS * (g - 1) + s, s)
                rest_of_tile(g, 1, 2)
                rest_of_tile(g, 1, 3)
                with dve.Fori(2, TURNS) as k:
                    for s in range(RING):
                        rest_of_tile(g, k, s)
            for j in range(BANKS):
                finish_chunk(BANKS * (GROUPS - 1) + j, j)

        @block.tensor
        def _(pe):
            def turn_rows(c, kept, norm, to, done):
                pe.wait_ge(norm, CHUNK * (c + 1))
                if not isinstance(c, int) or c:
                    pe.wait_ge(kept, c)
                for i in range(CHUNK):
                    last = pe.transpose(to[:, i * D:(i + 1) * D], hn[:, i, :], ident[:, :])
                last.then_inc(done, 1)

            def make_mh(c):
                pe.wait_ge(turned_kept, c + 1)
                if not isinstance(c, int) or c:
                    pe.wait_ge(mh_kept, c)
                for i in range(CHUNK):
                    last = pe.matmul(ps[1][:, i * D:(i + 1) * D], hT[:, i * D:(i + 1) * D], w_in_s[:, :],
                                     start=True, stop=True)
                last.then_inc(mh_made, 1)

            def sum_tile(g, k, s, start=False, stop=False):
                tile, turn = TILES * g + RING * k + s, TURNS * g + k
                pe.wait_ge(adj_in[s], 16 * (turn + 1))
                if s in SPLIT:
                    pe.wait_ge(hi_staged, turn + 1)
                    pe.wait_ge(lo_staged, turn + 1)
                    for h, (hi, lo) in enumerate(first_halves):
                        pe.wait_ge(hi_split, HALVES * turn + h + 1)
                        for n, (w, a) in enumerate(((stage_hi, hi), (stage_lo1, hi), (stage_hi, lo))):
                            if n == 2:
                                pe.wait_ge(lo_split, HALVES * turn + h + 1)
                            for j in range(2):
                                last = pe.matmul(acc[:, 2 * h + j, :], w[:, s, :], a[:, j, :],
                                                 start=False, stop=False)
                    last.then_inc(tile_summed, 1)
                    return
                pe.wait_ge(staged, (RING - len(SPLIT)) * turn + s + 1 - sum(x < s for x in SPLIT))
                for j in range(BANKS):
                    if start and g:
                        pe.wait_ge(m2n_kept, BANKS * (g - 1) + j + 1)
                    last = pe.matmul(acc[:, j, :], stage[:, s, :], ring[:, s, j * BANK:(j + 1) * BANK],
                                     start=start, stop=stop)
                last.then_inc(tile_summed, 1)

            pe.wait_ge(ident_ok, 1)
            turn_rows(0, turned_kept, rows_norm, ps[0], rows_turned)
            pe.wait_ge(win_in, 32)
            make_mh(0)

            def first_turn(k, make=True, first=False, end=False):
                if make:
                    turn_rows(k + 1, turned_kept, rows_norm, ps[0], rows_turned)
                for s in range(RING):
                    sum_tile(0, k, s, start=first and s == 0, stop=end and s == RING - 1)
                    if s == 1 and make:
                        make_mh(k + 1)

            def make_degrees(g):
                pe.wait_ge(deg_added, TILES * (g + 1))
                if g:
                    pe.wait_ge(deg_kept, g)
                for i in range(GROUP // P):
                    last = pe.matmul(ps[2][:, i:i + 1],
                                     degacc[g % 2][:, i // CHUNK, i % CHUNK * P:(i % CHUNK + 1) * P],
                                     ones[:, :], start=True, stop=True)
                last.then_inc(deg_made, 1)

            first_turn(0, first=True)
            with pe.Fori(1, TURNS - 1) as k:
                first_turn(k)
            first_turn(TURNS - 1, make=False, end=True)
            for g in range(1, GROUPS):
                for s in range(RING):
                    sum_tile(g, 0, s, start=s == 0)
                    if s == 0:
                        make_degrees(g - 1)
                with pe.Fori(1, TURNS - 1) as k:
                    for s in range(RING):
                        sum_tile(g, k, s)
                for s in range(RING):
                    sum_tile(g, TURNS - 1, s, stop=s == RING - 1)
            make_degrees(GROUPS - 1)
            pe.wait_ge(w_in_l, 16 * 10)

            pe.wait_ge(shift_ok, 1)
            for q in range(QT):
                for k in range(KT):
                    last = pe.matmul(ps[3][:, q:q + 1], w1_s[:, k, q * P:(q + 1) * P], bn_t[:, k:k + 1],
                                     start=k == 0, stop=k == KT - 1)
            last.then_inc(cvec_made, 1)
            pe.wait_ge(scaled_ok, 1)
            pe.wait_ge(m2n_kept, CHUNKS)

            def make_z(c, first=False):
                for q in range(QT):
                    if not first:
                        pe.wait_ge(z_biased, QT * (c - 1) + q + 1)
                    pe.matmul(ps[q][:, :], w1_s[:, 0, q * P:(q + 1) * P], nTs[:, cols(c), :].squeeze(1),
                              start=True, stop=False)
                    pe.matmul(ps[q][:, :], w1_s[:, 1, q * P:(q + 1) * P], m2nT[:, bass.ds(BANK * c, BANK)],
                              start=False, stop=True).then_inc(z_made, 1)

            make_z(0, first=True)
            with pe.Fori(1, CHUNKS) as c:
                make_z(c)

            pe.wait_ge(shift_ok, 2)
            pe.wait_ge(h_kept, CHUNKS * QT)
            for q in range(QT):
                last = pe.matmul(ps[3][:, 0:1], w2_s[:, q, :], bn_t[:, q:q + 1], start=q == 0, stop=q == QT - 1)
            last.then_inc(cvec_made, 1)
            pe.wait_ge(scaled_ok, 2)

            def make_y(c, first=False):
                if not first:
                    pe.wait_ge(y_biased, c)
                for q in range(QT):
                    last = pe.matmul(ps[2][:, :], w2_s[:, q, :], hid[:, cols(c), q, :].squeeze(1),
                                     start=q == 0, stop=q == QT - 1)
                last.then_inc(y_made, 1)

            def turn_y(c):
                pe.wait_ge(y_kept, c + 1)
                if not isinstance(c, int) or c:
                    pe.wait_ge(x1_made, c)
                for i in range(CHUNK):
                    last = pe.transpose(ps[0][:, i * D:(i + 1) * D], yT[:, i * P:(i + 1) * P], ident[:, :])
                last.then_inc(y_turned, 1)

            def make_support(c):
                pe.wait_ge(turned2_kept, c + 1)
                if not isinstance(c, int) or c:
                    pe.wait_ge(lo_kept, CHUNK * c)
                for i in range(CHUNK):
                    last = pe.matmul(ps[3][:, i * D:(i + 1) * D], hT[:, i * D:(i + 1) * D], w_s[:, :],
                                     start=True, stop=True)
                last.then_inc(sup_made, 1)

            def turn_rows2(c):
                turn_rows(c, turned2_kept, rows2_norm, ps[1], rows2_turned)

            make_y(0, first=True)
            turn_y(0)
            make_y(1)
            turn_y(1)
            turn_rows2(0)
            make_y(2)
            make_support(0)
            turn_y(2)
            turn_rows2(1)

            def sum_tile2(g, k, s, start=False, stop=False):
                tile = TILES * g + RING * k + s
                pe.wait_ge(staged2, 2 * tile + 2)
                for h in range(HALVES):
                    hi, lo = (halves[:, HALVES * (s % 2) + h, n] for n in range(2))
                    pe.wait_ge(split_hi, HALVES * tile + h + 1)
                    for n, (w, a) in enumerate(((stage_hi, hi), (stage_lo, hi), (stage_hi, lo))):
                        if n == 2:
                            pe.wait_ge(split_lo, HALVES * tile + h + 1)
                        for j in range(2):
                            if start and n == 0 and g:
                                pe.wait_ge(sum_kept, BANKS * (g - 1) + 2 * h + j + 1)
                            last = pe.matmul(acc[:, 2 * h + j, :], w[:, s, :], a[:, j, :],
                                             start=start and n == 0, stop=stop and n == 2)
                    last.then_inc(half_summed, 1)

            def turn_sums(c, j):
                pe.wait_ge(sum_kept, c + 1)
                if c >= BANKS:
                    pe.wait_ge(out_made, c - BANKS + 1)
                for i in range(CHUNK):
                    last = pe.transpose(ps[j][:, i * D:(i + 1) * D], sumT[:, j, i * P:(i + 1) * P], ident[:, :])
                last.then_inc(sum_turned, 1)

            def made_turn(k, start=False, stop=False, y=True, rows=True, support=True):
                sum_tile2(0, k, 0, start=start)
                if y:
                    make_y(k + 3)
                sum_tile2(0, k, 1)
                if support:
                    make_support(k + 1)
                sum_tile2(0, k, 2)
                if y:
                    turn_y(k + 3)
                sum_tile2(0, k, 3, stop=stop)
                if rows:
                    turn_rows2(k + 2)

            made_turn(0, start=True)
            with pe.Fori(1, TURNS - 3) as k:
                made_turn(k)
            made_turn(TURNS - 3, y=False)
            made_turn(TURNS - 2, y=False, rows=False)
            made_turn(TURNS - 1, stop=True, y=False, rows=False, support=False)
            for g in range(1, GROUPS):
                for s in range(RING):
                    sum_tile2(g, 0, s, start=s == 0)
                    turn_sums(BANKS * (g - 1) + s, s)
                with pe.Fori(1, TURNS - 1) as k:
                    for s in range(RING):
                        sum_tile2(g, k, s)
                for s in range(RING):
                    sum_tile2(g, TURNS - 1, s, stop=s == RING - 1)
            for j in range(BANKS):
                turn_sums(BANKS * (GROUPS - 1) + j, j)


def kernel(x, adj, L0_gnn_N, L0_gnn_W_in, L0_gnn_b_in, L0_gnn_g1, L0_gnn_be1, L0_gnn_W1, L0_gnn_b1,
           L0_gnn_g2, L0_gnn_be2, L0_gnn_W2, L0_gnn_b2, L1_gnn_weight, L1_gnn_bias):
    import numpy as np
    import concourse.bacc as bacc
    from concourse.bass_utils import run_bass_kernel_spmd

    def rows(a):
        return np.ascontiguousarray(np.asarray(a).reshape(TILES, P, D).transpose(1, 0, 2).reshape(P, NODES))

    def columns(a):
        return np.ascontiguousarray(np.asarray(a).reshape(-1, P).T)

    adjT = np.ascontiguousarray(
        np.asarray(adj).reshape(GROUPS, GROUP, TILES, P).transpose(0, 2, 3, 1).reshape(GROUPS * TILES, P, GROUP))
    arrays = {
        "adjT": adjT, "x_rows": rows(x), "n_rows": rows(L0_gnn_N),
        "nT": np.ascontiguousarray(np.asarray(L0_gnn_N).T),
        "w_inT": np.ascontiguousarray(np.asarray(L0_gnn_W_in).T), "b_in": np.asarray(L0_gnn_b_in),
        "g1": columns(L0_gnn_g1), "be1": columns(L0_gnn_be1),
        "w1T": np.ascontiguousarray(np.asarray(L0_gnn_W1).T), "b1": columns(L0_gnn_b1),
        "g2": columns(L0_gnn_g2), "be2": columns(L0_gnn_be2),
        "w2T": np.ascontiguousarray(np.asarray(L0_gnn_W2).T), "b2": columns(L0_gnn_b2),
        "weight": np.asarray(L1_gnn_weight), "bias": np.asarray(L1_gnn_bias),
    }
    nc = bacc.Bacc("TRN2", target_bir_lowering=False, num_devices=1, dynamic_dma_scratch_size=SCRATCH)
    args = [nc.dram_tensor(name, a.shape, F32, kind="ExternalInput").ap() for name, a in arrays.items()]
    out_rows = nc.dram_tensor("out_rows", (P, NODES), F32, kind="ExternalOutput").ap()
    gnn_kernel(nc, *args, out_rows)
    result = run_bass_kernel_spmd(nc, [arrays], core_ids=[0])
    got = result.results[0]["out_rows"]
    return got.reshape(P, TILES, D).transpose(1, 0, 2).reshape(NODES, D)
```

```python
from contextlib import ExitStack

import concourse.bass as bass
from concourse import mybir

F32 = mybir.dt.float32
F32R = mybir.dt.float32r
ALU = mybir.AluOpType
ACT = mybir.ActivationFunctionType

P = 128
D = 128
NODES = 8192
H = 512
EPS = 1e-5
SLOPE = 0.01

BANK = 512
GROUP = 2048
GROUPS = NODES // GROUP
BANKS = GROUP // BANK
TILES = NODES // P
CHUNK = BANK // P
CHUNKS = NODES // BANK
RING = 4
TURNS = TILES // RING
KT = 2 * D // P
QT = H // P
HALF = GROUP // 2
HALVES = 2
PAIRS = 4
SPLIT = (1,)
NT_PIECE = 4
ROW = 4 * BANK
SCRATCH = 1024


def gnn_kernel(nc, adjT, x_rows, n_rows, nT, w_inT, b_in, g1, be1, w1T, b1, g2, be2, w2T, b2,
               weight, bias, out_rows):
    with ExitStack() as ctx:
        top = [-(-nc.sbuf_base // 64) * 64]

        def at(name, shape, dt=F32, offset=None):
            size = 4
            for n in shape[1:]:
                size *= n
            if offset is None:
                offset = top[0]
                top[0] += -(-size // 32) * 32
            return nc.alloc_sbuf_tensor_at(name, shape, dt, offset=offset)

        ring = at("ring", [P, RING, GROUP])
        m2n_base = top[0]
        m2nT = at("m2nT", [P, NODES])
        m2n_lo = at("m2n_lo", [P, NODES], F32R, offset=m2n_base)
        halves = at("halves", [P, PAIRS, 2, 2, BANK], F32R, offset=m2n_base)
        space = top[0]
        hid = at("hid", [P, CHUNKS, QT, BANK])
        parts = at("parts", [P, CHUNKS, QT, BANK], F32R, offset=space)
        xr = hid[:, :, 3, :]
        nTs = hid[:, :, 1, :]
        degacc = [hid[:, 4 * b:4 * b + 4, 2, :] for b in range(2)]
        first_halves = [[parts[:, 8 + 4 * b + 2 * n:10 + 4 * b + 2 * n, 2, :] for n in range(2)]
                        for b in range(2)]
        sumT = hid[:, 0:BANKS, 3, :]

        def x1_chunk(c):
            return hid[:, bass.ds(c, 1), 2, :].squeeze(1)

        def x1_tile(c, i):
            return hid[:, bass.ds(c, 1), 2, i * D:(i + 1) * D].squeeze(1)

        def x_tile(c, i):
            return hid[:, bass.ds(c, 1), 3, i * D:(i + 1) * D].squeeze(1)

        def ring_half(s, h):
            return ring[:, s, h * HALF:(h + 1) * HALF].rearrange("p (a b) -> p a b", b=BANK)

        work = top[0]
        stage = at("stage", [P, RING, D])
        stage_lo1 = at("stage_lo1", [P, RING, D], F32R)
        stage_hi = at("stage_hi", [P, RING, D], F32R)
        stage_lo = at("stage_lo", [P, RING, D], F32R, offset=work)
        hn = at("hn", [P, CHUNK, D])
        hT = at("hT", [P, BANK])
        yT = at("yT", [P, BANK])
        at("room", [P, 3, BANK])
        w1_parts = [at("w1_n", [P, 2, H], F32R, offset=work + 3 * ROW),
                    at("w1_m2n", [P, 2, H], F32R, offset=work)]
        n_parts = at("n_parts", [P, 2, 2, BANK], F32R, offset=work + 5 * ROW)
        w2_scaled = at("w2_scaled", [P, QT, D], offset=work + 6 * ROW)

        bn2_base = top[0]
        bn2_st = at("bn2_st", [P, QT, CHUNKS, 6])
        w_in_s = at("w_in_s", [P, D], offset=bn2_base)
        b_in_s = at("b_in_s", [P, D], offset=bn2_base + 4 * D)
        w1_s = at("w1_s", [P, KT, H])
        w2_s = at("w2_s", [P, QT, D])
        w_s = at("w_s", [P, D])
        ident = at("ident", [P, P])
        bias_s = at("bias_s", [P, D])
        g1_s = at("g1_s", [P, KT])
        be1_s = at("be1_s", [P, KT])
        b1_s = at("b1_s", [P, QT])
        g2_s = at("g2_s", [P, QT])
        be2_s = at("be2_s", [P, QT])
        b2_s = at("b2_s", [P, 1])
        ones = at("ones", [P, 1])
        mhalf = at("mhalf", [P, CHUNK])
        ln_bn = at("ln_bn", [P, CHUNK, 6])
        ln_mv = at("ln_mv", [P, CHUNK, 2])
        ln_neg = at("ln_neg", [P, TILES])
        ln_ve = at("ln_ve", [P, TILES])
        ln_rs = at("ln_rs", [P, TILES])
        ln_sh = at("ln_sh", [P, TILES])
        bn1_st = at("bn1_st", [P, KT, CHUNKS, 6])
        bn_mv = at("bn_mv", [P, QT, 2])
        bn_ve = at("bn_ve", [P, QT])
        bn_rs = at("bn_rs", [P, QT])
        bn_s = at("bn_s", [P, QT])
        bn_ms = at("bn_ms", [P, QT])
        bn_t = at("bn_t", [P, QT])
        c1 = at("c1", [P, QT])
        c2 = at("c2", [P, 1])
        tick = at("tick", [P, 1])
        deg = at("deg", [P, TILES])
        dzero = at("dzero", [P, TILES])
        dinv = at("dinv", [P, TILES])
        dsc = at("dsc", [P, TILES])
        assert top[0] <= nc.sbuf_top, top[0]

        acc = ctx.enter_context(nc.psum_tensor("acc", [P, BANKS, BANK], F32))
        ps = [ctx.enter_context(nc.psum_tensor(f"ps{i}", [P, BANK], F32)) for i in range(4)]

        def sem(name):
            return ctx.enter_context(nc.semaphore(name))

        win_in, w_in_l, xn_in, stored = (
            sem(n) for n in ("win_in", "w_in_l", "xn_in", "stored"))
        x_in = [sem(f"x_in{i}") for i in range(4)]
        nT_in = [sem(f"nT_in{i}") for i in range(CHUNKS // NT_PIECE)]
        xn_first = [sem(f"xn_first{c}") for c in range(4)]
        adj_in = [sem(f"adj_in{s}") for s in range(RING)]
        const_ok, ident_ok = sem("const_ok"), sem("ident_ok")
        ln_part, ln_var, ln_rstd, ln_shift = sem("ln_part"), sem("ln_var"), sem("ln_rstd"), sem("ln_shift")
        rows_norm, rows_turned, turned_kept, mh_made, mh_kept = (
            sem(n) for n in ("rows_norm", "rows_turned", "turned_kept", "mh_made", "mh_kept"))
        staged, tile_summed, deg_added = sem("staged"), sem("tile_summed"), sem("deg_added")
        hi_staged, lo_staged, hi_split, lo_split = (
            sem(n) for n in ("hi_staged", "lo_staged", "hi_split", "lo_split"))
        m2n_kept, deg_made, deg_kept, bn1_seen = (
            sem(n) for n in ("m2n_kept", "deg_made", "deg_kept", "bn1_seen"))
        dve_step, pool_step = sem("dve_step"), sem("pool_step")
        m2n_hi_ok, m2n_lo_ok, w1_hi_ok, w1_lo_ok, n_hi_ok, n_lo_ok, n_used = (
            sem(n) for n in ("m2n_hi_ok", "m2n_lo_ok", "w1_hi_ok", "w1_lo_ok", "n_hi_ok",
                             "n_lo_ok", "n_used"))
        bn_var, bn_rstd, shift_ok, cvec_made, scaled_ok = (
            sem(n) for n in ("bn_var", "bn_rstd", "shift_ok", "cvec_made", "scaled_ok"))
        z_made, z_biased, h_kept, h_seen = sem("z_made"), sem("z_biased"), sem("h_kept"), sem("h_seen")
        y_made, y_biased, y_kept, y_turned, xn_made, x1_made = (
            sem(n) for n in ("y_made", "y_biased", "y_kept", "y_turned", "xn_made", "x1_made"))
        deg_final, d_ok, w2_ok = sem("deg_final"), sem("d_ok"), sem("w2_ok")
        ln2_var, ln2_rstd, ln2_shift = sem("ln2_var"), sem("ln2_rstd"), sem("ln2_shift")
        rows2_norm, rows2_turned, turned2_kept, sup_made, hi_kept, lo_kept = (
            sem(n) for n in ("rows2_norm", "rows2_turned", "turned2_kept", "sup_made", "hi_kept", "lo_kept"))
        bias_added = sem("bias_added")
        staged2, split_hi, split_lo, half_summed = (
            sem(n) for n in ("staged2", "split_hi", "split_lo", "half_summed"))
        sum_kept, sum_turned, out_made = sem("sum_kept"), sem("sum_turned"), sem("out_made")

        PASS = GROUPS * TILES
        x_pieces = ((0, 2), (2, 4), (4, 10), (10, CHUNKS))

        def cols(t, n=1):
            return bass.ds(t, n)

        block = ctx.enter_context(nc.Block())

        @block.sync
        def _(sp):
            xr_d = x_rows.rearrange("p (c j) -> p c j", j=BANK)
            def load_x(i):
                a, b = x_pieces[i]
                sp.dma_start(xr[:, a:b, :], xr_d[:, a:b, :]).then_inc(x_in[i], 16)

            def load_tile(tile, s):
                sp.dma_start(ring[:, s, :], adjT[tile]).then_inc(adj_in[s], 16)

            load_x(0)
            sp.dma_start(w_in_s[:, :], w_inT).then_inc(win_in, 16)
            sp.dma_start(b_in_s[:, :], b_in.partition_broadcast(P)).then_inc(win_in, 16)
            load_tile(0, 0)
            load_x(1)
            load_tile(1, 1)
            load_tile(2, 2)
            load_x(2)
            load_tile(3, 3)

            def next_turn(k):
                for s in range(RING):
                    sp.wait_ge(tile_summed, RING * (k - 1) + s + 1)
                    sp.wait_ge(deg_added, RING * (k - 1) + s + 1)
                    load_tile(RING * k + s, s)

            next_turn(1)
            load_x(3)
            with sp.Fori(2, TURNS // 2) as k:
                next_turn(k)
            sp.dma_start(w1_s[:, :, :], w1T.rearrange("(k p) h -> p k h", p=P)).then_inc(w_in_l, 16)
            sp.dma_start(w2_s[:, :, :], w2T.rearrange("(k p) h -> p k h", p=P)).then_inc(w_in_l, 16)
            sp.dma_start(w_s[:, :], weight).then_inc(w_in_l, 16)
            sp.dma_start(bias_s[:, :], bias.partition_broadcast(P)).then_inc(w_in_l, 16)
            for dst, src in ((g1_s, g1), (be1_s, be1), (b1_s, b1), (g2_s, g2), (be2_s, be2), (b2_s, b2)):
                sp.dma_start(dst[:, :], src).then_inc(w_in_l, 16)
            with sp.Fori(TURNS // 2, TURNS) as k:
                next_turn(k)
            for i, a in enumerate(range(0, CHUNKS, NT_PIECE)):
                next_turn(TURNS + 2 * i)
                sp.dma_start(nTs[:, a:a + NT_PIECE, :], nT.rearrange("p (c j) -> p c j", j=BANK)[
                    :, a:a + NT_PIECE, :]).then_inc(nT_in[i], 16)
                next_turn(TURNS + 2 * i + 1)
            with sp.Fori(TURNS + 2 * CHUNKS // NT_PIECE, PASS // RING) as k:
                next_turn(k)
            for s in range(RING):
                sp.wait_ge(tile_summed, PASS - RING + s + 1)
                sp.wait_ge(deg_added, PASS - RING + s + 1)
                load_tile(s, s)
            for c in range(4):
                sp.wait_ge(y_made, c + 1)
                sp.dma_start(x1_chunk(c), xr_d[:, c, :]).then_inc(xn_first[c], 16)
                sp.dma_start(hid[:, c, 3, :], n_rows.rearrange("p (c j) -> p c j", j=BANK)[:, c, :])\
                    .then_inc(xn_first[c], 16)
            with sp.Fori(1, PASS // RING) as k:
                for s in range(RING):
                    sp.wait_ge(split_lo, HALVES * (RING * (k - 1) + s + 1))
                    load_tile(RING * k + s, s)
            with sp.Fori(0, CHUNKS) as c:
                sp.wait_ge(out_made, c + 1)
                sp.dma_start(out_rows.rearrange("p (c j) -> p c j", j=BANK)[:, bass.ds(c, 1), :].squeeze(1),
                             x1_chunk(c)).then_inc(stored, 16)
            sp.wait_ge(stored, 16 * CHUNKS)

        @block.gpsimd
        def _(pool):
            pool.memset(ident[:, :], 0.0).then_inc(const_ok, 1)
            pool.memset(ones[:, :], 1.0).then_inc(const_ok, 1)
            pool.memset(mhalf[:, :], -0.5).then_inc(const_ok, 1)
            pool.wait_ge(const_ok, 3)
            pool.affine_select(out=ident[:, :], in_=ident[:, :], compare_op=ALU.not_equal, fill=1.0,
                               base=0, pattern=[[-1, P]], channel_multiplier=1).then_inc(ident_ok, 1)

            def row_scales(c, var, rstd, shift):
                at4 = cols(CHUNK * c, CHUNK)
                pool.wait_ge(var, c + 1)
                pool.tensor_tensor(ln_rs[:, at4], ln_ve[:, at4], mhalf[:, :], ALU.pow).then_inc(rstd, 1)
                pool.wait_ge(rstd, c + 1)
                pool.tensor_tensor(ln_sh[:, at4], ln_neg[:, at4], ln_rs[:, at4], ALU.mult).then_inc(shift, 1)

            with pool.Fori(0, CHUNKS) as c:
                row_scales(c, ln_var, ln_rstd, ln_shift)

            for k in range(KT):
                pool.wait_ge(bn_var, k + 1)
                pool.tensor_tensor(bn_rs[:, k:k + 1], bn_ve[:, k:k + 1], mhalf[:, 0:1], ALU.pow).then_inc(bn_rstd, 1)
            pool.wait_ge(deg_final, 1)
            with pool.Fori(0, CHUNKS) as c:
                at4 = cols(CHUNK * c, CHUNK)
                pool.tensor_tensor(dinv[:, at4], deg[:, at4], mhalf[:, :], ALU.pow).then_inc(pool_step, 1)
            pool.wait_ge(bn_var, KT + 1)
            pool.tensor_tensor(bn_rs[:, :], bn_ve[:, :], mhalf[:, 0:QT], ALU.pow).then_inc(bn_rstd, 1)
            def add_rows(c):
                if isinstance(c, int) and c < 4:
                    pool.wait_ge(xn_first[c], 32)
                else:
                    pool.wait_ge(xn_in, 32 * (c - 3))
                pool.tensor_tensor(x1_chunk(c), x1_chunk(c), hid[:, cols(c), 3, :].squeeze(1),
                                   ALU.add).then_inc(xn_made, 1)

            def add_bias(c):
                pool.wait_ge(rows2_norm, CHUNK * (c + 1))
                pool.tensor_tensor(x1_chunk(c).rearrange("p (i d) -> p i d", d=D),
                                   x1_chunk(c).rearrange("p (i d) -> p i d", d=D),
                                   bias_s[:, :].unsqueeze(1).broadcast_to([P, CHUNK, D]),
                                   ALU.add).then_inc(bias_added, 1)

            add_rows(0)
            add_rows(1)
            for c in (2, 3):
                row_scales(c - 2, ln2_var, ln2_rstd, ln2_shift)
                add_rows(c)
            row_scales(2, ln2_var, ln2_rstd, ln2_shift)
            add_bias(0)
            add_bias(1)
            with pool.Fori(4, CHUNKS) as c:
                row_scales(c - 1, ln2_var, ln2_rstd, ln2_shift)
                add_rows(c)
                add_bias(c - 2)
            row_scales(CHUNKS - 1, ln2_var, ln2_rstd, ln2_shift)
            add_bias(CHUNKS - 2)
            add_bias(CHUNKS - 1)

        @block.scalar
        def _(act):
            def normalise(c, rows, shift, done, turned):
                act.wait_ge(shift, c + 1)
                if turned is not None:
                    act.wait_ge(turned, c)
                for i in range(CHUNK):
                    t = CHUNK * c + i
                    act.activation(hn[:, i, :], rows(c, i), ACT.Relu, bias=ln_sh[:, cols(t)],
                                   scale=ln_rs[:, cols(t)]).then_inc(done, 1)

            def keep_turned(c):
                act.wait_ge(rows_turned, c + 1)
                if not isinstance(c, int) or c:
                    act.wait_ge(mh_made, c)
                act.activation(hT[:, :], ps[0][:, :], ACT.Copy).then_inc(turned_kept, 1)

            def mh_tile(t, s):
                return hid[:, cols(t), 0, s * D:(s + 1) * D].squeeze(1)

            def feed_tile(g, k, s, first=False):
                tile = TILES * g + RING * k + s
                if not first:
                    act.wait_ge(tile_summed, tile - RING + 1)
                if s not in SPLIT:
                    act.activation(stage[:, s, :], mh_tile(k, s), ACT.Copy).then_inc(staged, 1)
                    return
                act.activation(stage_hi[:, s, :], mh_tile(k, s), ACT.Copy).then_inc(hi_staged, 1)
                act.wait_ge(adj_in[s], 16 * (TURNS * g + k + 1))
                for h in range(HALVES):
                    act.activation(first_halves[h][0], ring_half(s, h), ACT.Copy).then_inc(hi_split, 1)

            def first_turn(k, first=False, ahead=True, make=True):
                act.wait_ge(mh_kept, k + 1)
                for s in range(RING):
                    feed_tile(0, k, s, first)
                    if s == 1 and make:
                        keep_turned(k + 1)
                    if s == 2 and ahead:
                        normalise(k + 2, x_tile, ln_shift, rows_norm, rows_turned)

            def keep_group(g):
                act.wait_ge(tile_summed, TILES * (g + 1))
                for j in range(BANKS):
                    act.activation(m2nT[:, bass.ds(GROUP * g + BANK * j, BANK)], acc[:, j, :],
                                   ACT.Copy).then_inc(m2n_kept, 1)

            normalise(0, x_tile, ln_shift, rows_norm, None)
            keep_turned(0)
            normalise(1, x_tile, ln_shift, rows_norm, None)
            first_turn(0, first=True)
            with act.Fori(1, TURNS - 2) as k:
                first_turn(k)
            first_turn(TURNS - 2, ahead=False)
            first_turn(TURNS - 1, ahead=False, make=False)

            def split_m2n(c):
                act.wait_ge(m2n_kept, c + 1)
                act.activation(parts[:, c, 3, :], m2nT[:, c * BANK:(c + 1) * BANK], ACT.Copy)\
                    .then_inc(m2n_hi_ok, 1)

            def split_w1(k):
                act.wait_ge(shift_ok, k + 1)
                act.activation(w1_parts[k][:, 0, :], w1_s[:, k, :], ACT.Copy,
                               scale=bn_s[:, k:k + 1]).then_inc(w1_hi_ok, 1)

            def split_n(c, b):
                if not isinstance(c, int) or c >= 2:
                    act.wait_ge(n_used, c - 1)
                act.activation(n_parts[:, b, 0, :], nTs[:, cols(c), :].squeeze(1), ACT.Copy).then_inc(n_hi_ok, 1)

            for g in range(1, GROUPS):
                for s in range(RING - 1):
                    feed_tile(g, 0, s)
                keep_group(g - 1)
                feed_tile(g, 0, RING - 1)
                for s in range(RING):
                    feed_tile(g, 1, s)
                    split_m2n(BANKS * (g - 1) + s)
                with act.Fori(2, TURNS) as k:
                    for s in range(RING):
                        feed_tile(g, k, s)
                if g == GROUPS - 2:
                    split_w1(0)
            for c in range(2):
                split_n(c, c)
            keep_group(GROUPS - 1)
            split_w1(1)
            for j in range(BANKS):
                split_m2n(BANKS * (GROUPS - 1) + j)

            act.wait_ge(scaled_ok, 1)

            def keep_z(c):
                for q in range(QT):
                    act.wait_ge(z_made, QT * c + q + 1)
                    act.activation(hid[:, cols(c), q, :].squeeze(1), ps[q][:, :], ACT.Identity,
                                   bias=c1[:, q:q + 1]).then_inc(z_biased, 1)

            with act.Fori(0, CHUNKS - 3, 2) as c:
                for b in range(2):
                    keep_z(c + b)
                    split_n(c + b + 2, b)
            keep_z(CHUNKS - 2)
            keep_z(CHUNKS - 1)

            def keep_y(c):
                act.wait_ge(y_made, c + 1)
                if not isinstance(c, int) or c:
                    act.wait_ge(y_turned, c)
                bank = acc[:, c, :] if isinstance(c, int) and 1 <= c < 4 else ps[2][:, :]
                act.activation(yT[:, :], bank, ACT.Identity, bias=c2[:, 0:1]).then_inc(y_biased, 1)
                if isinstance(c, int) and c < 4:
                    return
                act.wait_ge(xn_made, c)
                act.dma_start(x1_chunk(c), x_rows.rearrange("p (c j) -> p c j", j=BANK)[
                    :, cols(c), :].squeeze(1)).then_inc(xn_in, 16)
                act.dma_start(hid[:, cols(c), 3, :].squeeze(1), n_rows.rearrange("p (c j) -> p c j", j=BANK)[
                    :, cols(c), :].squeeze(1)).then_inc(xn_in, 16)

            def keep_hi(c):
                act.wait_ge(sup_made, c + 1)
                for i in range(CHUNK):
                    act.activation(parts[:, cols(c), 0, i * D:(i + 1) * D].squeeze(1),
                                   ps[3][:, i * D:(i + 1) * D], ACT.Copy,
                                   scale=dsc[:, cols(CHUNK * c + i)]).then_inc(hi_kept, 1)

            act.wait_ge(scaled_ok, 2)
            keep_y(0)
            keep_y(1)
            keep_y(2)
            normalise(0, x1_tile, ln2_shift, rows2_norm, None)
            normalise(1, x1_tile, ln2_shift, rows2_norm, rows2_turned)
            keep_y(3)
            act.wait_ge(d_ok, 1)
            keep_hi(0)

            def split_tile(g, k, s, first=False):
                tile = TILES * g + RING * k + s
                if not first:
                    act.wait_ge(half_summed, HALVES * (tile - RING + 1))
                for n, to in enumerate((stage_hi, stage_lo)):
                    act.activation(to[:, s, :], parts[:, cols(k), n, s * D:(s + 1) * D].squeeze(1).bitcast(F32),
                                   ACT.Copy).then_inc(staged2, 1)
                act.wait_ge(adj_in[s], 16 * (TURNS * (GROUPS + g) + k + 1))
                for h in range(HALVES):
                    pair = HALVES * (s % 2) + h
                    if not (first and s < 2):
                        act.wait_ge(half_summed, HALVES * tile + h - PAIRS + 1)
                    act.activation(halves[:, pair, 0], ring_half(s, h), ACT.Copy).then_inc(split_hi, 1)

            def made_turn(k, first=False, y=True, norm=True, support=True):
                act.wait_ge(lo_kept, CHUNK * (k + 1))
                split_tile(0, k, 0, first)
                if support:
                    keep_hi(k + 1)
                split_tile(0, k, 1, first)
                if first:
                    normalise(k + 2, x1_tile, ln2_shift, rows2_norm, rows2_turned)
                split_tile(0, k, 2, first)
                split_tile(0, k, 3, first)
                if y:
                    keep_y(k + 4)
                if norm:
                    normalise(k + 3, x1_tile, ln2_shift, rows2_norm, rows2_turned)

            made_turn(0, first=True)
            with act.Fori(1, TURNS - 4) as k:
                made_turn(k)
            made_turn(TURNS - 4, y=False)
            made_turn(TURNS - 3, y=False, norm=False)
            made_turn(TURNS - 2, y=False, norm=False)
            made_turn(TURNS - 1, y=False, norm=False, support=False)

            def keep_sums(g):
                for j in range(BANKS):
                    if j % 2 == 0:
                        act.wait_ge(half_summed, HALVES * (TILES * (g + 1) - 1) + j // 2 + 1)
                    if g:
                        act.wait_ge(sum_turned, BANKS * (g - 1) + j + 1)
                    act.activation(sumT[:, j, :], acc[:, j, :], ACT.Copy).then_inc(sum_kept, 1)

            for g in range(1, GROUPS):
                split_tile(g, 0, 0)
                keep_sums(g - 1)
                for s in range(1, RING):
                    split_tile(g, 0, s)
                with act.Fori(1, TURNS) as k:
                    for s in range(RING):
                        split_tile(g, k, s)
            keep_sums(GROUPS - 1)

        @block.vector
        def _(dve):
            steps = [0]

            def step(ins):
                steps[0] += 1
                ins.then_inc(dve_step, 1)
                dve.wait_ge(dve_step, steps[0])

            def plain():
                dve.wait_ge(const_ok, 3)

            def carry():
                dve.tensor_copy(tick[:, :], ones[:, :])

            def row_stats(c, rows, part, var, first=False):
                plain()
                if not isinstance(c, int) or c:
                    dve.wait_ge(part, 3 * c)
                    dve.wait_ge(var, c)
                    carry()
                for i in range(CHUNK):
                    last = dve.bn_stats(ln_bn[:, i, :], rows(c, i))
                last.then_inc(part, 1)
                dve.wait_ge(part, 3 * c + 1)
                carry()
                for i in range(CHUNK):
                    last = dve.bn_aggr(ln_mv[:, i, :], ln_bn[:, i, :])
                last.then_inc(part, 1)
                dve.wait_ge(part, 3 * c + 2)
                at4 = cols(CHUNK * c, CHUNK)
                dve.tensor_scalar(ln_neg[:, at4], ln_mv[:, :, 0], -1.0, None, ALU.mult).then_inc(part, 1)
                dve.tensor_scalar(ln_ve[:, at4], ln_mv[:, :, 1], EPS, None, ALU.add).then_inc(var, 1)

            def keep_mh(c):
                dve.wait_ge(mh_made, c + 1)
                dve.tensor_tensor(hid[:, cols(c), 0, :].squeeze(1).rearrange("p (i d) -> p i d", d=D),
                                  ps[1][:, :].rearrange("p (i d) -> p i d", d=D),
                                  b_in_s[:, :].unsqueeze(1).broadcast_to([P, CHUNK, D]),
                                  ALU.add).then_inc(mh_kept, 1)

            def rest_of_mh(g, k):
                for s in SPLIT:
                    dve.wait_ge(hi_staged, TURNS * g + k + 1)
                    dve.tensor_tensor(stage_lo1[:, s, :], hid[:, cols(k), 0, s * D:(s + 1) * D].squeeze(1),
                                      stage_hi[:, s, :].bitcast(F32), ALU.subtract).then_inc(lo_staged, 1)

            def add_tile(g, k, s):
                tile, sums = TILES * g + RING * k + s, degacc[g % 2]
                dve.wait_ge(adj_in[s], 16 * (TURNS * g + k + 1))
                if isinstance(k, int) and k == 0 and s == 0:
                    if g >= 2:
                        dve.wait_ge(deg_made, g - 1)
                    dve.tensor_copy(sums, ring[:, s, :].rearrange("p (a b) -> p a b", b=BANK)).then_inc(deg_added, 1)
                else:
                    if s in SPLIT:
                        for h in range(HALVES):
                            dve.wait_ge(hi_split, HALVES * (TURNS * g + k) + h + 1)
                            dve.tensor_tensor(first_halves[h][1], ring_half(s, h),
                                              first_halves[h][0].bitcast(F32), ALU.subtract).then_inc(lo_split, 1)
                    dve.wait_ge(deg_added, tile)
                    dve.tensor_tensor(sums, sums, ring[:, s, :].rearrange("p (a b) -> p a b", b=BANK),
                                      ALU.add).then_inc(deg_added, 1)

            dve.wait_ge(x_in[0], 16)
            row_stats(0, x_tile, ln_part, ln_var)
            row_stats(1, x_tile, ln_part, ln_var)
            dve.wait_ge(win_in, 32)
            keep_mh(0)
            dve.wait_ge(x_in[1], 16)
            row_stats(2, x_tile, ln_part, ln_var)

            def first_turn(k, make=True, stats=True):
                rest_of_mh(0, k)
                for s in range(RING):
                    add_tile(0, k, s)
                    if s == 1 and make:
                        keep_mh(k + 1)
                if stats:
                    row_stats(k + 3, x_tile, ln_part, ln_var)

            def keep_degrees(g):
                dve.wait_ge(deg_made, g + 1)
                dve.tensor_copy(deg[:, bass.ds(GROUP // P * g, GROUP // P)],
                                ps[2][:, 0:GROUP // P]).then_inc(deg_kept, 1)

            def m2n_stats(c):
                dve.wait_ge(m2n_kept, c + 1)
                dve.bn_stats(bn1_st[:, 1, c, :], m2nT[:, c * BANK:(c + 1) * BANK]).then_inc(bn1_seen, 1)

            def nT_stats(c):
                dve.bn_stats(bn1_st[:, 0, c, :], nTs[:, c, :]).then_inc(bn1_seen, 1)

            first_turn(0)
            dve.wait_ge(x_in[2], 16)
            with dve.Fori(1, x_pieces[3][0] - 3) as k:
                first_turn(k)
            dve.wait_ge(x_in[3], 16)
            with dve.Fori(x_pieces[3][0] - 3, CHUNKS - 3) as k:
                first_turn(k)
            first_turn(CHUNKS - 3, stats=False)
            first_turn(CHUNKS - 2, stats=False)
            first_turn(CHUNKS - 1, make=False, stats=False)

            def rest_of_m2n(c):
                dve.wait_ge(m2n_hi_ok, c + 1)
                dve.wait_ge(bn1_seen, (0 if c < BANKS else CHUNKS) + c + 1)
                dve.tensor_tensor(m2n_lo[:, c * BANK:(c + 1) * BANK], m2nT[:, c * BANK:(c + 1) * BANK],
                                  parts[:, c, 3, :].bitcast(F32), ALU.subtract).then_inc(m2n_lo_ok, 1)

            def rest_of_n(c, b):
                dve.wait_ge(n_hi_ok, c + 1)
                dve.tensor_tensor(n_parts[:, b, 1, :], nTs[:, cols(c), :].squeeze(1),
                                  n_parts[:, b, 0, :].bitcast(F32), ALU.subtract).then_inc(n_lo_ok, 1)

            def bn_moments(st, k, count):
                step(dve.bn_aggr(bn_mv[:, k, :], st[:, k, :, :].rearrange("p c s -> p (c s)")))
                dve.tensor_scalar(bn_ve[:, k:k + 1], bn_mv[:, k, 1:2], EPS, None, ALU.add).then_inc(count, 1)

            def bn_shift(k, gamma, beta, rstd, use_scale=None):
                dve.wait_ge(bn_rstd, rstd)
                step(dve.tensor_tensor(bn_s[:, k], bn_rs[:, k], gamma[:, k], ALU.mult))
                if use_scale:
                    use_scale()
                step(dve.tensor_tensor(bn_ms[:, k], bn_mv[:, k, 0], bn_s[:, k], ALU.mult))
                dve.tensor_tensor(bn_t[:, k], beta[:, k], bn_ms[:, k], ALU.subtract).then_inc(shift_ok, 1)

            def rest_of_w1(k):
                dve.wait_ge(w1_hi_ok, k + 1)
                dve.scalar_tensor_tensor(out=w1_parts[k][:, 1, :], in0=w1_s[:, k, :], scalar=bn_s[:, k:k + 1],
                                         in1=w1_parts[k][:, 0, :].bitcast(F32), op0=ALU.mult,
                                         op1=ALU.subtract).then_inc(w1_lo_ok, 1)

            for g in range(1, GROUPS):
                rest_of_mh(g, 0)
                for s in range(RING):
                    add_tile(g, 0, s)
                    if s == 1:
                        keep_degrees(g - 1)
                rest_of_mh(g, 1)
                for s in range(RING):
                    add_tile(g, 1, s)
                    m2n_stats(BANKS * (g - 1) + s)
                for k in range(2, 3 + CHUNKS // 2):
                    rest_of_mh(g, k)
                    for s in range(RING):
                        add_tile(g, k, s)
                        if k == 2:
                            rest_of_m2n(BANKS * (g - 1) + s)
                        elif g == 1 and s % 2:
                            c = 2 * (k - 3) + s // 2
                            if c % NT_PIECE == 0:
                                dve.wait_ge(nT_in[c // NT_PIECE], 16)
                            nT_stats(c)
                if g == 2:
                    dve.wait_ge(w_in_l, 16 * 10)
                    dve.wait_ge(bn1_seen, CHUNKS + BANKS * 2)
                    bn_moments(bn1_st, 0, bn_var)
                    bn_shift(slice(0, 1), g1_s, be1_s, 1)
                with dve.Fori(3 + CHUNKS // 2, TURNS) as k:
                    rest_of_mh(g, k)
                    for s in range(RING):
                        add_tile(g, k, s)
                if g == 2:
                    rest_of_w1(0)
            for c in range(2):
                rest_of_n(c, c)
            keep_degrees(GROUPS - 1)
            for j in range(BANKS):
                m2n_stats(BANKS * (GROUPS - 1) + j)

            dve.wait_ge(bn1_seen, 2 * CHUNKS)
            bn_moments(bn1_st, 1, bn_var)
            bn_shift(slice(1, 2), g1_s, be1_s, 2)
            rest_of_w1(1)
            dve.wait_ge(cvec_made, 1)
            dve.tensor_tensor(c1[:, :], acc[:, 0, 0:QT], b1_s[:, :], ALU.add).then_inc(scaled_ok, 1)
            for j in range(BANKS):
                rest_of_m2n(BANKS * (GROUPS - 1) + j)
            dve.wait_ge(deg_kept, GROUPS)
            step(dve.tensor_scalar(dzero[:, :], deg[:, :], 0.0, None, ALU.is_equal))
            dve.tensor_tensor(deg[:, :], deg[:, :], dzero[:, :], ALU.add).then_inc(deg_final, 1)

            def leaky(u):
                return dve.scalar_tensor_tensor(out=u, in0=u, scalar=SLOPE, in1=u, op0=ALU.mult, op1=ALU.max)

            def keep_h(c):
                for q in range(QT + 1):
                    if q < QT:
                        dve.wait_ge(z_biased, QT * c + q + 1)
                        leaky(hid[:, cols(c), q, :].squeeze(1)).then_inc(h_kept, 1)
                    if q:
                        plain()
                        dve.wait_ge(h_kept, QT * c + q)
                        dve.bn_stats(bn2_st[:, q - 1, cols(c), :].squeeze(1),
                                     hid[:, cols(c), q - 1, :].squeeze(1)).then_inc(h_seen, 1)

            with dve.Fori(0, CHUNKS - 3, 2) as c:
                for b in range(2):
                    keep_h(c + b)
                    rest_of_n(c + b + 2, b)
            keep_h(CHUNKS - 2)
            keep_h(CHUNKS - 1)
            def scale_w2():
                dve.wait_ge(n_used, CHUNKS)
                for q in range(QT):
                    dve.tensor_scalar(w2_scaled[:, q, :], w2_s[:, q, :], bn_s[:, q:q + 1], None,
                                      ALU.mult).then_inc(w2_ok, 1)

            dve.wait_ge(h_seen, CHUNKS * QT)
            for k in range(QT):
                last = dve.bn_aggr(bn_mv[:, k, :], bn2_st[:, k, :, :].rearrange("p c s -> p (c s)"))
            step(last)
            dve.tensor_scalar(bn_ve[:, :], bn_mv[:, :, 1], EPS, None, ALU.add).then_inc(bn_var, 1)
            bn_shift(slice(0, QT), g2_s, be2_s, KT + 1, scale_w2)
            dve.wait_ge(cvec_made, 2)
            dve.tensor_tensor(c2[:, :], acc[:, 0, 0:1], b2_s[:, :], ALU.add).then_inc(scaled_ok, 1)

            def leave_y(c):
                dve.wait_ge(y_biased, c + 1)
                leaky(yT[:, :]).then_inc(y_kept, 1)

            def make_x1(c):
                dve.wait_ge(xn_made, c + 1)
                dve.wait_ge(y_turned, c + 1)
                dve.tensor_tensor(x1_chunk(c), x1_chunk(c), ps[0][:, :], ALU.add).then_inc(x1_made, 1)
                plain()
                dve.wait_ge(x1_made, c + 1)
                dve.wait_ge(ln_part, 3 * (CHUNKS + c))
                if isinstance(c, int) and c == 0:
                    dve.wait_ge(ln_var, CHUNKS)
                else:
                    dve.wait_ge(ln2_var, c)
                carry()
                for i in range(CHUNK):
                    last = dve.bn_stats(ln_bn[:, i, :], x1_tile(c, i))
                last.then_inc(ln_part, 1)
                dve.wait_ge(ln_part, 3 * (CHUNKS + c) + 1)
                carry()
                for i in range(CHUNK):
                    last = dve.bn_aggr(ln_mv[:, i, :], ln_bn[:, i, :])
                last.then_inc(ln_part, 1)
                dve.wait_ge(ln_part, 3 * (CHUNKS + c) + 2)
                at4 = cols(CHUNK * c, CHUNK)
                dve.tensor_scalar(ln_neg[:, at4], ln_mv[:, :, 0], -1.0, None, ALU.mult).then_inc(ln_part, 1)
                dve.tensor_scalar(ln_ve[:, at4], ln_mv[:, :, 1], EPS, None, ALU.add).then_inc(ln2_var, 1)

            def keep_turned2(c):
                dve.wait_ge(rows2_turned, c + 1)
                if not isinstance(c, int) or c:
                    dve.wait_ge(sup_made, c)
                dve.tensor_copy(hT[:, :], ps[1][:, :]).then_inc(turned2_kept, 1)

            def keep_lo(c):
                dve.wait_ge(hi_kept, CHUNK * (c + 1))
                for i in range(CHUNK):
                    dve.scalar_tensor_tensor(
                        out=parts[:, cols(c), 1, i * D:(i + 1) * D].squeeze(1),
                        in0=ps[3][:, i * D:(i + 1) * D], scalar=dsc[:, cols(CHUNK * c + i)],
                        in1=parts[:, cols(c), 0, i * D:(i + 1) * D].squeeze(1).bitcast(F32),
                        op0=ALU.mult, op1=ALU.subtract).then_inc(lo_kept, 1)

            leave_y(0)
            dve.wait_ge(pool_step, CHUNKS)
            step(dve.tensor_tensor(dzero[:, :], dinv[:, :], dzero[:, :], ALU.mult))
            dve.tensor_tensor(dsc[:, :], dinv[:, :], dzero[:, :], ALU.subtract).then_inc(d_ok, 1)
            dve.wait_ge(d_ok, 1)
            make_x1(0)
            leave_y(1)
            make_x1(1)
            leave_y(2)
            keep_turned2(0)
            make_x1(2)
            leave_y(3)
            keep_turned2(1)
            keep_lo(0)

            def rest_of_tile(g, k, s):
                tile = TILES * g + RING * k + s
                for h in range(HALVES):
                    pair = HALVES * (s % 2) + h
                    dve.wait_ge(split_hi, HALVES * tile + h + 1)
                    dve.tensor_tensor(halves[:, pair, 1], ring_half(s, h),
                                      halves[:, pair, 0].bitcast(F32), ALU.subtract).then_inc(split_lo, 1)

            def made_turn(k, y=True, x1=True, turned=True, support=True):
                rest_of_tile(0, k, 0)
                if support:
                    keep_lo(k + 1)
                rest_of_tile(0, k, 1)
                rest_of_tile(0, k, 2)
                if x1:
                    make_x1(k + 3)
                if turned:
                    keep_turned2(k + 2)
                rest_of_tile(0, k, 3)
                if y:
                    leave_y(k + 4)

            def finish_chunk(c, j):
                dve.wait_ge(sum_turned, c + 1)
                dve.wait_ge(bias_added, c + 1)
                for i in range(CHUNK):
                    last = dve.scalar_tensor_tensor(
                        out=x1_tile(c, i), in0=ps[j][:, i * D:(i + 1) * D], scalar=dsc[:, cols(CHUNK * c + i)],
                        in1=x1_tile(c, i), op0=ALU.mult, op1=ALU.add)
                last.then_inc(out_made, 1)

            with dve.Fori(0, TURNS - 4) as k:
                made_turn(k)
            made_turn(TURNS - 4, y=False)
            made_turn(TURNS - 3, y=False, x1=False)
            made_turn(TURNS - 2, y=False, x1=False, turned=False)
            made_turn(TURNS - 1, y=False, x1=False, turned=False, support=False)
            for g in range(1, GROUPS):
                rest_of_tile(g, 0, 0)
                rest_of_tile(g, 0, 1)
                for s in range(RING):
                    rest_of_tile(g, (s + 2) // RING, (s + 2) % RING)
                    finish_chunk(BANKS * (g - 1) + s, s)
                rest_of_tile(g, 1, 2)
                rest_of_tile(g, 1, 3)
                with dve.Fori(2, TURNS) as k:
                    for s in range(RING):
                        rest_of_tile(g, k, s)
            for j in range(BANKS):
                finish_chunk(BANKS * (GROUPS - 1) + j, j)

        @block.tensor
        def _(pe):
            def turn_rows(c, kept, norm, to, done):
                pe.wait_ge(norm, CHUNK * (c + 1))
                if not isinstance(c, int) or c:
                    pe.wait_ge(kept, c)
                for i in range(CHUNK):
                    last = pe.transpose(to[:, i * D:(i + 1) * D], hn[:, i, :], ident[:, :])
                last.then_inc(done, 1)

            def make_mh(c):
                pe.wait_ge(turned_kept, c + 1)
                if not isinstance(c, int) or c:
                    pe.wait_ge(mh_kept, c)
                for i in range(CHUNK):
                    last = pe.matmul(ps[1][:, i * D:(i + 1) * D], hT[:, i * D:(i + 1) * D], w_in_s[:, :],
                                     start=True, stop=True)
                last.then_inc(mh_made, 1)

            def sum_tile(g, k, s, start=False, stop=False):
                tile, turn = TILES * g + RING * k + s, TURNS * g + k
                pe.wait_ge(adj_in[s], 16 * (turn + 1))
                if s in SPLIT:
                    pe.wait_ge(hi_staged, turn + 1)
                    for h, (hi, lo) in enumerate(first_halves):
                        pe.wait_ge(hi_split, HALVES * turn + h + 1)
                        for n, (w, a) in enumerate(((stage_hi, hi), (stage_lo1, hi), (stage_hi, lo))):
                            if n == 1 and h == 0:
                                pe.wait_ge(lo_staged, turn + 1)
                            if n == 2:
                                pe.wait_ge(lo_split, HALVES * turn + h + 1)
                            for j in range(2):
                                last = pe.matmul(acc[:, 2 * h + j, :], w[:, s, :], a[:, j, :],
                                                 start=False, stop=False)
                    last.then_inc(tile_summed, 1)
                    return
                pe.wait_ge(staged, (RING - len(SPLIT)) * turn + s + 1 - sum(x < s for x in SPLIT))
                for j in range(BANKS):
                    if start and g:
                        pe.wait_ge(m2n_kept, BANKS * (g - 1) + j + 1)
                    last = pe.matmul(acc[:, j, :], stage[:, s, :], ring[:, s, j * BANK:(j + 1) * BANK],
                                     start=start, stop=stop)
                last.then_inc(tile_summed, 1)

            pe.wait_ge(ident_ok, 1)
            turn_rows(0, turned_kept, rows_norm, ps[0], rows_turned)
            pe.wait_ge(win_in, 32)
            make_mh(0)

            def first_turn(k, make=True, first=False, end=False):
                if make:
                    turn_rows(k + 1, turned_kept, rows_norm, ps[0], rows_turned)
                for s in range(RING):
                    sum_tile(0, k, s, start=first and s == 0, stop=end and s == RING - 1)
                    if s == 1 and make:
                        make_mh(k + 1)

            def make_degrees(g):
                pe.wait_ge(deg_added, TILES * (g + 1))
                if g:
                    pe.wait_ge(deg_kept, g)
                for i in range(GROUP // P):
                    last = pe.matmul(ps[2][:, i:i + 1],
                                     degacc[g % 2][:, i // CHUNK, i % CHUNK * P:(i % CHUNK + 1) * P],
                                     ones[:, :], start=True, stop=True)
                last.then_inc(deg_made, 1)

            first_turn(0, first=True)
            with pe.Fori(1, TURNS - 1) as k:
                first_turn(k)
            first_turn(TURNS - 1, make=False, end=True)
            for g in range(1, GROUPS):
                for s in range(RING):
                    sum_tile(g, 0, s, start=s == 0)
                    if s == 0:
                        make_degrees(g - 1)
                with pe.Fori(1, TURNS - 1) as k:
                    for s in range(RING):
                        sum_tile(g, k, s)
                for s in range(RING):
                    sum_tile(g, TURNS - 1, s, stop=s == RING - 1)
            make_degrees(GROUPS - 1)

            def add_z(c, q, k, hi, lo):
                w_hi, w_lo = (w1_parts[k][:, n, q * P:(q + 1) * P] for n in range(2))
                pe.matmul(ps[q][:, :], w_hi, hi, start=k == 0, stop=False)
                pe.matmul(ps[q][:, :], w_lo, hi, start=False, stop=False)
                return pe.matmul(ps[q][:, :], w_hi, lo, start=False, stop=k == KT - 1)

            def z_of_n(c, b, first=False):
                pe.wait_ge(n_lo_ok, c + 1)
                for q in range(QT):
                    if not first:
                        pe.wait_ge(z_biased, QT * (c - 1) + q + 1)
                    last = add_z(c, q, 0, n_parts[:, b, 0, :], n_parts[:, b, 1, :])
                last.then_inc(n_used, 1)

            def z_of_m2n(c):
                pe.wait_ge(m2n_lo_ok, c + 1)
                for q in range(QT):
                    add_z(c, q, 1, parts[:, cols(c), 3, :].squeeze(1),
                          m2n_lo[:, bass.ds(BANK * c, BANK)]).then_inc(z_made, 1)

            pe.wait_ge(w1_lo_ok, 1)
            pe.wait_ge(deg_kept, GROUPS)
            z_of_n(0, 0, first=True)
            pe.wait_ge(m2n_kept, CHUNKS)
            pe.wait_ge(shift_ok, 2)
            for q in range(QT):
                for k in range(KT):
                    last = pe.matmul(acc[:, 0, q:q + 1], w1_s[:, k, q * P:(q + 1) * P], bn_t[:, k:k + 1],
                                     start=k == 0, stop=k == KT - 1)
            last.then_inc(cvec_made, 1)
            pe.wait_ge(w1_lo_ok, 2)
            z_of_m2n(0)
            z_of_n(1, 1)
            z_of_m2n(1)
            with pe.Fori(2, CHUNKS - 1, 2) as c:
                for b in range(2):
                    z_of_n(c + b, b)
                    z_of_m2n(c + b)

            def y_bank(c):
                return acc[:, c, :] if isinstance(c, int) and 1 <= c < 4 else ps[2][:, :]

            def make_y(c):
                if not isinstance(c, int) or c >= 4:
                    pe.wait_ge(y_biased, c)
                for q in range(QT):
                    if isinstance(c, int) and c == 0:
                        pe.wait_ge(w2_ok, q + 1)
                    last = pe.matmul(y_bank(c), w2_scaled[:, q, :], hid[:, cols(c), q, :].squeeze(1),
                                     start=q == 0, stop=q == QT - 1)
                last.then_inc(y_made, 1)

            pe.wait_ge(z_biased, QT * CHUNKS)
            make_y(0)
            pe.wait_ge(shift_ok, 3)
            for q in range(QT):
                last = pe.matmul(acc[:, 0, 0:1], w2_s[:, q, :], bn_t[:, q:q + 1], start=q == 0, stop=q == QT - 1)
            last.then_inc(cvec_made, 1)

            def turn_y(c):
                pe.wait_ge(y_kept, c + 1)
                if not isinstance(c, int) or c:
                    pe.wait_ge(x1_made, c)
                for i in range(CHUNK):
                    last = pe.transpose(ps[0][:, i * D:(i + 1) * D], yT[:, i * P:(i + 1) * P], ident[:, :])
                last.then_inc(y_turned, 1)

            def make_support(c):
                pe.wait_ge(turned2_kept, c + 1)
                if not isinstance(c, int) or c:
                    pe.wait_ge(lo_kept, CHUNK * c)
                for i in range(CHUNK):
                    last = pe.matmul(ps[3][:, i * D:(i + 1) * D], hT[:, i * D:(i + 1) * D], w_s[:, :],
                                     start=True, stop=True)
                last.then_inc(sup_made, 1)

            def turn_rows2(c):
                turn_rows(c, turned2_kept, rows2_norm, ps[1], rows2_turned)

            make_y(1)
            turn_y(0)
            make_y(2)
            turn_y(1)
            make_y(3)
            turn_rows2(0)
            turn_y(2)
            make_support(0)
            turn_rows2(1)
            turn_y(3)
            make_support(1)
            pe.wait_ge(y_biased, 4)
            pe.wait_ge(scaled_ok, 2)

            def sum_tile2(g, k, s, start=False, stop=False):
                tile = TILES * g + RING * k + s
                pe.wait_ge(staged2, 2 * tile + 2)
                for h in range(HALVES):
                    hi, lo = (halves[:, HALVES * (s % 2) + h, n] for n in range(2))
                    pe.wait_ge(split_hi, HALVES * tile + h + 1)
                    for n, (w, a) in enumerate(((stage_hi, hi), (stage_lo, hi), (stage_hi, lo))):
                        if n == 2:
                            pe.wait_ge(split_lo, HALVES * tile + h + 1)
                        for j in range(2):
                            if start and n == 0 and g:
                                pe.wait_ge(sum_kept, BANKS * (g - 1) + 2 * h + j + 1)
                            last = pe.matmul(acc[:, 2 * h + j, :], w[:, s, :], a[:, j, :],
                                             start=start and n == 0, stop=stop and n == 2)
                    last.then_inc(half_summed, 1)

            def turn_sums(c, j):
                pe.wait_ge(sum_kept, c + 1)
                if c >= BANKS:
                    pe.wait_ge(out_made, c - BANKS + 1)
                for i in range(CHUNK):
                    last = pe.transpose(ps[j][:, i * D:(i + 1) * D], sumT[:, j, i * P:(i + 1) * P], ident[:, :])
                last.then_inc(sum_turned, 1)

            def made_turn(k, start=False, stop=False, y=True, rows=True, support=True):
                sum_tile2(0, k, 0, start=start)
                if y:
                    make_y(k + 4)
                sum_tile2(0, k, 1)
                if start:
                    turn_rows2(k + 2)
                sum_tile2(0, k, 2)
                if support:
                    make_support(k + 2)
                sum_tile2(0, k, 3, stop=stop)
                if y:
                    turn_y(k + 4)
                if rows:
                    turn_rows2(k + 3)

            made_turn(0, start=True)
            with pe.Fori(1, TURNS - 4) as k:
                made_turn(k)
            made_turn(TURNS - 4, y=False)
            made_turn(TURNS - 3, y=False, rows=False)
            made_turn(TURNS - 2, y=False, rows=False, support=False)
            made_turn(TURNS - 1, stop=True, y=False, rows=False, support=False)
            for g in range(1, GROUPS):
                for s in range(RING):
                    sum_tile2(g, 0, s, start=s == 0)
                    turn_sums(BANKS * (g - 1) + s, s)
                with pe.Fori(1, TURNS - 1) as k:
                    for s in range(RING):
                        sum_tile2(g, k, s)
                for s in range(RING):
                    sum_tile2(g, TURNS - 1, s, stop=s == RING - 1)
            for j in range(BANKS):
                turn_sums(BANKS * (GROUPS - 1) + j, j)


def kernel(x, adj, L0_gnn_N, L0_gnn_W_in, L0_gnn_b_in, L0_gnn_g1, L0_gnn_be1, L0_gnn_W1, L0_gnn_b1,
           L0_gnn_g2, L0_gnn_be2, L0_gnn_W2, L0_gnn_b2, L1_gnn_weight, L1_gnn_bias):
    import numpy as np
    import concourse.bacc as bacc
    from concourse.bass_utils import run_bass_kernel_spmd

    def rows(a):
        return np.ascontiguousarray(np.asarray(a).reshape(TILES, P, D).transpose(1, 0, 2).reshape(P, NODES))

    def columns(a):
        return np.ascontiguousarray(np.asarray(a).reshape(-1, P).T)

    adjT = np.ascontiguousarray(
        np.asarray(adj).reshape(GROUPS, GROUP, TILES, P).transpose(0, 2, 3, 1).reshape(GROUPS * TILES, P, GROUP))
    arrays = {
        "adjT": adjT, "x_rows": rows(x), "n_rows": rows(L0_gnn_N),
        "nT": np.ascontiguousarray(np.asarray(L0_gnn_N).T),
        "w_inT": np.ascontiguousarray(np.asarray(L0_gnn_W_in).T), "b_in": np.asarray(L0_gnn_b_in),
        "g1": columns(L0_gnn_g1), "be1": columns(L0_gnn_be1),
        "w1T": np.ascontiguousarray(np.asarray(L0_gnn_W1).T), "b1": columns(L0_gnn_b1),
        "g2": columns(L0_gnn_g2), "be2": columns(L0_gnn_be2),
        "w2T": np.ascontiguousarray(np.asarray(L0_gnn_W2).T), "b2": columns(L0_gnn_b2),
        "weight": np.asarray(L1_gnn_weight), "bias": np.asarray(L1_gnn_bias),
    }
    nc = bacc.Bacc("TRN2", target_bir_lowering=False, num_devices=1, dynamic_dma_scratch_size=SCRATCH)
    args = [nc.dram_tensor(name, a.shape, F32, kind="ExternalInput").ap() for name, a in arrays.items()]
    out_rows = nc.dram_tensor("out_rows", (P, NODES), F32, kind="ExternalOutput").ap()
    gnn_kernel(nc, *args, out_rows)
    result = run_bass_kernel_spmd(nc, [arrays], core_ids=[0])
    got = result.results[0]["out_rows"]
    return got.reshape(P, TILES, D).transpose(1, 0, 2).reshape(NODES, D)
```
